# Optimizing a Trainium2 kernel written in Bass

```python
import numpy as np
import jax
import jax.numpy as jnp

def _softmax(x, axis=-1):
    return jax.nn.softmax(x, axis=axis)

def _gelu(x):
    return jax.nn.gelu(x, approximate=True)

def _silu(x):
    return jax.nn.silu(x)

def _sigmoid(x):
    return jax.nn.sigmoid(x)

def _layernorm(x, axis=-1, eps=1e-05):
    m = jnp.mean(x, axis=axis, keepdims=True)
    v = jnp.var(x, axis=axis, keepdims=True)
    return (x - m) / jnp.sqrt(v + eps)

def _scatter_add(tgt, idx, src, axis=0):
    return tgt.at[idx].add(src)

def _segment_sum(src, seg, n):
    return jax.ops.segment_sum(src, seg, n)
kernel_name = 'mk_adaln_ffn_d1_seqx_r4_2280d0'

def setup_inputs(seed: int=0):
    np.random.seed(seed)
    _w = jnp.asarray

    def _rec_inputs():
        import jax
        import jax.numpy as jnp
        _rk = jax.random.key(seed)
        x = 8.748e-05 + 1 * jax.random.normal(jax.random.fold_in(_rk, 1), (64, 64, 512), jnp.float32)
        _lenS = 64 - jax.random.randint(jax.random.fold_in(_rk, 7), (64,), 0, max(1, 64 // 4) + 1, jnp.int32)
        _lenS2 = 64 - jax.random.randint(jax.random.fold_in(_rk, 8), (64,), 0, max(1, 64 // 4) + 1, jnp.int32)
        cond_2048 = -9.80646e-05 + 1.00041 * jax.random.normal(jax.random.fold_in(_rk, 11), (64, 512), jnp.float32)
        return (x, cond_2048)
    x, cond_2048 = _rec_inputs()

    def _L0_cond_setup():
        import jax, jax.numpy as jnp
        import numpy as np
        DT = 0.01
        EPSILON = 0.08
        ALPHA = 0.7
        BETA = 0.8
        CLAMP = 20.0
        B, T, N = (64, 128, 512)

        def _derivative(q, p, drive, coupling, bias):
            i_couple = jnp.tanh(q) @ coupling.T
            dq = q - q ** 3 / 3.0 - p + drive + i_couple + bias
            dp = EPSILON * (q + ALPHA - BETA * p)
            return (dq, dp)

        def _rk4_step(q, p, drive, coupling, bias):
            dq1, dp1 = _derivative(q, p, drive, coupling, bias)
            dq2, dp2 = _derivative(q + 0.5 * DT * dq1, p + 0.5 * DT * dp1, drive, coupling, bias)
            dq3, dp3 = _derivative(q + 0.5 * DT * dq2, p + 0.5 * DT * dp2, drive, coupling, bias)
            dq4, dp4 = _derivative(q + DT * dq3, p + DT * dp3, drive, coupling, bias)
            q_next = q + DT / 6.0 * (dq1 + 2 * dq2 + 2 * dq3 + dq4)
            p_next = p + DT / 6.0 * (dp1 + 2 * dp2 + 2 * dp3 + dp4)
            q_next = jnp.clip(q_next, -CLAMP, CLAMP)
            p_next = jnp.clip(p_next, -CLAMP, CLAMP)
            return (q_next, p_next)
        key = jax.random.key(seed)
        k1, k2, k3, k4 = jax.random.split(key, 4)
        return {'q0': jax.random.normal(k1, (B, N), dtype=jnp.float32), 'p0': jax.random.normal(k2, (B, N), dtype=jnp.float32), 'input_drive_seq': jax.random.normal(k3, (B, T, N), dtype=jnp.float32), 'coupling': jax.random.normal(k4, (N, N), dtype=jnp.float32) * 0.01, 'bias': jnp.zeros((N,), dtype=jnp.float32)}
    _L0_cond_all = _L0_cond_setup()
    _L0_cond_in = {k: v for k, v in _L0_cond_all.items() if k in ('coupling', 'bias')}
    del _L0_cond_all

    def _L0_ffn_setup():
        import jax, jax.numpy as jnp
        import numpy as np
        TOPK = 2
        N_EXPERTS = 8
        ROUTE_SCALE = 1.0
        key = jax.random.key(seed)
        ks = jax.random.split(key, 7)
        B, T, C = (4, 512, 512)
        H = 352
        HS = 704
        E = N_EXPERTS
        s = 0.02
        return {'x': jax.random.normal(ks[0], (B, T, C), jnp.float32), 'gate_w': jax.random.normal(ks[1], (E, C), jnp.float32) * s, 'gate_bias': jnp.zeros((E,), jnp.float32), 'shared_gw': jax.random.normal(ks[2], (2 * HS, C), jnp.float32) * s, 'shared_dw': jax.random.normal(ks[3], (C, HS), jnp.float32) * s, 'up_w': jax.random.normal(ks[4], (E, 2 * H, C), jnp.float32) * s, 'down_w': jax.random.normal(ks[5], (E, C, H), jnp.float32) * s}
    _L0_ffn_all = _L0_ffn_setup()
    _L0_ffn_in = {k: v for k, v in _L0_ffn_all.items() if k in ('gate_w', 'gate_bias', 'shared_gw', 'shared_dw', 'up_w', 'down_w')}
    del _L0_ffn_all
    return {'x': x, 'cond_2048': cond_2048, 'L0_cond_coupling': _L0_cond_in['coupling'], 'L0_cond_bias': _L0_cond_in['bias'], 'L0_ffn_gate_w': _L0_ffn_in['gate_w'], 'L0_ffn_gate_bias': _L0_ffn_in['gate_bias'], 'L0_ffn_shared_gw': _L0_ffn_in['shared_gw'], 'L0_ffn_shared_dw': _L0_ffn_in['shared_dw'], 'L0_ffn_up_w': _L0_ffn_in['up_w'], 'L0_ffn_down_w': _L0_ffn_in['down_w']}

def reference(x, cond_2048, L0_cond_coupling, L0_cond_bias, L0_ffn_gate_w, L0_ffn_gate_bias, L0_ffn_shared_gw, L0_ffn_shared_dw, L0_ffn_up_w, L0_ffn_down_w):
    import jax
    import jax.numpy as jnp

    def _L0_cond_ref(q0, p0, input_drive_seq, coupling, bias):
        import jax, jax.numpy as jnp
        import numpy as np
        DT = 0.01
        EPSILON = 0.08
        ALPHA = 0.7
        BETA = 0.8
        CLAMP = 20.0
        B, T, N = (64, 128, 512)

        def _derivative(q, p, drive, coupling, bias):
            i_couple = jnp.tanh(q) @ coupling.T
            dq = q - q ** 3 / 3.0 - p + drive + i_couple + bias
            dp = EPSILON * (q + ALPHA - BETA * p)
            return (dq, dp)

        def _rk4_step(q, p, drive, coupling, bias):
            dq1, dp1 = _derivative(q, p, drive, coupling, bias)
            dq2, dp2 = _derivative(q + 0.5 * DT * dq1, p + 0.5 * DT * dp1, drive, coupling, bias)
            dq3, dp3 = _derivative(q + 0.5 * DT * dq2, p + 0.5 * DT * dp2, drive, coupling, bias)
            dq4, dp4 = _derivative(q + DT * dq3, p + DT * dp3, drive, coupling, bias)
            q_next = q + DT / 6.0 * (dq1 + 2 * dq2 + 2 * dq3 + dq4)
            p_next = p + DT / 6.0 * (dp1 + 2 * dp2 + 2 * dp3 + dp4)
            q_next = jnp.clip(q_next, -CLAMP, CLAMP)
            p_next = jnp.clip(p_next, -CLAMP, CLAMP)
            return (q_next, p_next)
        drive_tbn = jnp.swapaxes(input_drive_seq, 0, 1)

        def scan_fn(carry, drive):
            q, p = carry
            q, p = _rk4_step(q, p, drive, coupling, bias)
            return ((q, p), q)
        (_, _), q_trace_tbn = jax.lax.scan(scan_fn, (q0, p0), drive_tbn)
        return jnp.swapaxes(q_trace_tbn, 0, 1)

    def _L0_ffn_ref(x, gate_w, gate_bias, shared_gw, shared_dw, up_w, down_w):
        import jax, jax.numpy as jnp
        import numpy as np
        TOPK = 2
        N_EXPERTS = 8
        ROUTE_SCALE = 1.0
        B, T, C = x.shape
        xf = x.reshape(-1, C)
        yg = xf @ shared_gw.T
        y, g = jnp.split(yg, 2, axis=-1)
        shared = jax.nn.silu(g) * y @ shared_dw.T
        scores = jax.nn.sigmoid(xf @ gate_w.T)
        _, topk_idx = jax.lax.top_k(scores + gate_bias, TOPK)
        w = jnp.take_along_axis(scores, topk_idx, axis=-1)
        w = w / jnp.sum(w, axis=-1, keepdims=True) * ROUTE_SCALE
        out = jnp.zeros_like(xf)
        for e in range(N_EXPERTS):
            we = jnp.sum(jnp.where(topk_idx == e, w, 0.0), axis=-1)
            gu = xf @ up_w[e].T
            g_e, u_e = jnp.split(gu, 2, axis=-1)
            h = jax.nn.silu(g_e) * u_e
            out = out + h @ down_w[e].T * we[:, None]
        return (shared + out).reshape(B, T, C)
    x = x + _L0_ffn_ref(_L0_cond_ref(cond_2048, cond_2048, x, L0_cond_coupling, L0_cond_bias), L0_ffn_gate_w, L0_ffn_gate_bias, L0_ffn_shared_gw, L0_ffn_shared_dw, L0_ffn_up_w, L0_ffn_down_w)
    return x

_drawn_inputs = setup_inputs


def setup_inputs(seed=0):
    import zlib

    import numpy as np

    out = dict(_drawn_inputs(seed))
    spreads = {'L0_cond_bias': (0.0, 0.8), 'L0_ffn_gate_bias': (0.0, 0.452)}
    factors = {'L0_cond_coupling': 8.0,
     'L0_ffn_gate_w': 3.994,
     'L0_ffn_up_w': 2.968,
     'L0_ffn_down_w': 3.002}
    for name, (base, spread) in spreads.items():
        noise = np.random.default_rng([zlib.crc32(name.encode()), seed]).standard_normal(out[name].shape)
        drawn = base * np.exp(spread * noise) if base else spread * noise
        out[name] = jnp.asarray(drawn.astype(out[name].dtype))
    for name, factor in factors.items():
        out[name] = (out[name] * factor).astype(out[name].dtype)
    return out
```

```python
from contextlib import ExitStack

import numpy as np

import concourse.bass as bass
from concourse import mybir

F32 = mybir.dt.float32
F16 = mybir.dt.float16
ACT = mybir.ActivationFunctionType
ALU = mybir.AluOpType
AXIS = mybir.AxisListType

P = 128
B, T, N = 64, 64, 512
NC = N // P
E = 8
H = 352
NW = E + 2
TOK = P
STEPS = TOK // B
TILES = B * T // TOK
STAGES = 4
GS = STEPS * STAGES
UPC = 2 * H
UP = NC * UPC
HK = [(0, 128), (128, 128), (256, 96)]
DOWN = len(HK) * N
WC = UP + DOWN

DT = 0.01
EPS = 0.08
ALPHA = 0.7
BETA = 0.8
CLAMP = 20.0
SHIFT = ALPHA / BETA

SW = 2.0 ** 8
SX = 2.0 ** 11
ST = 2.0 ** 15
SH = 2.0 ** 4
STEP = [DT / 2, DT / 2, DT, DT / 6]

JOBS = NW
ORDER = [E, E + 1] + list(range(E))
AT_STAGE = [[0], [1], [2, 3], [4], [5], [6, 7], [8], [9]]


def at(it, per_tile, tile, local=0):
    if it is None:
        return per_tile * tile + local
    return it * (2 * per_tile) + (per_tile * tile + local)


def build(nc, drive, cond, rows, coupling, bias, gate, gate_bias, up, down, out):
    with ExitStack() as ctx:
        def sb(name, shape, dt=F32):
            return ctx.enter_context(nc.sbuf_tensor(name, shape, dt))

        def pb(name, shape, dt=F32):
            return ctx.enter_context(nc.psum_tensor(name, shape, dt))

        def sem(name):
            return ctx.enter_context(nc.semaphore(name))

        w = sb("w", [P, NW, 2, WC], F16)
        cw = sb("cw", [P, 2, NC, N], F16)
        gw = sb("gw", [P, 2, NC, E], F16)
        gb = sb("gb", [P, E])
        bias_sb = sb("bias_sb", [P, NC])
        q = [sb(f"q{i}", [P, NC, B]) for i in range(STAGES)]
        p = [sb(f"p{i}", [P, NC, B]) for i in range(STAGES)]
        base = sb("base", [P, NC, B])
        vel = sb("vel", [P, NC, B])
        ref = sb("ref", [P, NC, B])
        sq = sb("sq", [P, NC, B])
        tanh = sb("tanh", [P, NC, B])
        th = sb("th", [P, 2, NC, B], F16)
        drv = [sb(f"drv{i}", [P, NC, B]) for i in range(2)]
        qp = [sb(f"qp{i}", [P, 2, NC, TOK], F16) for i in range(2)]
        hid = sb("hid", [P, H])
        ht = sb("ht", [P, 2, len(HK), TOK], F16)
        acc = [sb(f"acc{i}", [P, N]) for i in range(2)]
        ident = sb("ident", [P, P])
        desc = sb("desc", [P, E])
        r = {k: sb("r_" + k, [P, E]) for k in ("sc", "z", "zt", "lo", "sel", "k1", "o1", "k2", "o2", "wt")}
        m = {k: sb("m_" + k, [P, 1]) for k in ("m1", "i1", "m2", "i2", "den", "rd")}

        ps_rk = pb("ps_rk", [P, NC, B])
        ps_g = pb("ps_g", [P, 512])
        ps_u = pb("ps_u", [P, 512])
        ps_t = pb("ps_t", [P, len(HK), P])
        ps_y = pb("ps_y", [P, N])
        ps_l = pb("ps_l", [P, 512])

        names = ("bias_rdy cond_in consts_in ident_rdy stage_in0 stage_in1 w_hi w_lo c_in "
                 "tanh_rdy th_rdy tl_rdy sq_rdy rk_mm cubic_rdy slope_rdy ref_rdy base_rdy next_raw q_rdy "
                 "v_rdy v_rdy2 p_rdy drv_in0 drv_in1 d_rdy d_used qsum_rdy psum_rdy qh_rdy qp_rdy "
                 "up_mm sg_rdy h_rdy ht_mm hth_rdy hts_rdy y_mm y_done lg_mm sc_rdy route route_rdy "
                 "acc_in0 acc_in1 out0 out1").split()
        s = {n: sem(n) for n in names}

        def stages(h):
            return [(i, i // STAGES, i % STAGES) for i in range(GS)]

        stage_buf = [acc[0], acc[1]]
        pieces = []
        for k in range(NC):
            pieces.append((coupling[:, k, :], P, N, cw[:, 0, k, :], cw[:, 1, k, :]))
        pieces.append((gate, P, NC * E, gw[:, 0, :, :].rearrange("p a b -> p (a b)"),
                       gw[:, 1, :, :].rearrange("p a b -> p (a b)")))
        for e in ORDER:
            for c in range(0, UP, N):
                n = min(N, UP - c)
                pieces.append((up[e, :, c:c + n], P, n, w[:, e, 0, c:c + n], w[:, e, 1, c:c + n]))
            for k, (h0, hn) in enumerate(HK):
                c = UP + k * N
                pieces.append((down[e, h0:h0 + hn, :], hn, N, w[0:hn, e, 0, c:c + N], w[0:hn, e, 1, c:c + N]))
        NP = len(pieces)

        block = ctx.enter_context(nc.Block())

        @block.sync
        def _(sp):
            sp.dma_start(q[0][:], cond).then_inc(s["cond_in"], 16)
            sp.dma_start(bias_sb[:], bias).then_inc(s["consts_in"], 16)
            sp.dma_start(gb[:], gate_bias.rearrange("(a n) -> a n", a=1).to_broadcast([P, E])).then_inc(s["consts_in"], 16)
            for t in range(2):
                sp.dma_start(drv[t][:], drive[t]).then_inc(s[f"drv_in{t}"], 16)
            for n, (src, pp, cols, _, _) in enumerate(pieces):
                if n >= 2:
                    sp.wait_ge(s["w_lo"], n - 1)
                sp.dma_start(stage_buf[n % 2][0:pp, 0:cols], src).then_inc(s[f"stage_in{n % 2}"], 16)
            sp.wait_ge(s["w_lo"], NP)

            def drives(it, tile):
                for st in range(STEPS):
                    sp.wait_ge(s["d_used"], at(it, STEPS, tile, st + 1))
                    t = at(it, STEPS, tile, st + 2)
                    src = drive[t] if it is None else drive[bass.ds(t, 1)].rearrange("o p c b -> (o p) c b")
                    sp.dma_start(drv[st][:], src).then_inc(s[f"drv_in{st}"], 16)

            def result_out(it, tile, par):
                sp.wait_ge(s["y_done"], at(it, JOBS, tile, JOBS))
                r0 = at(it, TOK, tile)
                dst = out[bass.ds(r0, TOK), :] if it is not None else out[r0:r0 + TOK, :]
                sp.dma_start(dst, acc[par][:]).then_inc(s[f"out{par}"], 16)

            def residual_in(it, tile, par, first=False):
                if not first:
                    sp.wait_ge(s[f"out{par}"], at(it, 8, tile - par))
                r0 = at(it, TOK, tile)
                src = rows[bass.ds(r0, TOK), :] if it is not None else rows[r0:r0 + TOK, :]
                sp.dma_start(acc[par][:], src).then_inc(s[f"acc_in{par}"], 16)

            residual_in(None, 0, 0, first=True)
            residual_in(None, 1, 1, first=True)
            drives(None, 0)
            with sp.Fori(0, TILES // 2 - 1) as it:
                for h in range(2):
                    drives(it, 1 + h)
                    result_out(it, h, h)
                    residual_in(it, h + 2, h)
            result_out(None, TILES - 2, 0)
            result_out(None, TILES - 1, 1)
            sp.wait_ge(s["out0"], 16 * TILES // 2)
            sp.wait_ge(s["out1"], 16 * TILES // 2)

        @block.gpsimd
        def _(pool):
            pool.memset(ident[:], 0.0).then_inc(s["ident_rdy"], 1)
            pool.wait_ge(s["ident_rdy"], 1)
            pool.affine_select(out=ident[:], in_=ident[:], compare_op=ALU.not_equal, fill=1.0, base=0,
                               pattern=[[-1, P]], channel_multiplier=1).then_inc(s["ident_rdy"], 1)
            for e in range(E):
                pool.memset(desc[:, e:e + 1], float(E - e)).then_inc(s["ident_rdy"], 1)
            pool.wait_ge(s["consts_in"], 32)
            pool.tensor_scalar(bias_sb[:], bias_sb[:], -SHIFT, None, ALU.add).then_inc(s["bias_rdy"], 1)
            pool.wait_ge(s["bias_rdy"], 1)

            def drives(it, tile):
                for st in range(STEPS):
                    pool.wait_ge(s[f"drv_in{st}"], at(it, 16, tile, 16))
                    pool.tensor_tensor(drv[st][:], drv[st][:],
                                       bias_sb[:].rearrange("p (c o) -> p c o", o=1).to_broadcast([P, NC, B]),
                                       ALU.add).then_inc(s["d_rdy"], 1)
            drives(None, 0)
            with pool.Fori(0, TILES // 2 - 1) as it:
                for h in range(2):
                    drives(it, 1 + h)
            drives(None, TILES - 1)

        @block.scalar
        def _(act):
            def tanh_of(it, tile, i, src):
                g = (GS, tile, i)
                act.wait_ge(s["q_rdy"], at(it, *g) + 1)
                act.activation(tanh[:], src[:], ACT.Tanh).then_inc(s["tanh_rdy"], 1)
                act.activation(sq[:], src[:], ACT.Square, scale=3.0 ** -0.5).then_inc(s["sq_rdy"], 1)
                act.wait_ge(s["tanh_rdy"], at(it, *g) + 1)
                act.activation(th[:, 0], tanh[:], ACT.Copy, scale=ST).then_inc(s["th_rdy"], 1)

            tanh_of(None, 0, 0, q[0])
            for n, (_, pp, cols, hi, _) in enumerate(pieces):
                act.wait_ge(s[f"stage_in{n % 2}"], 16 * (n // 2 + 1))
                act.activation(hi, stage_buf[n % 2][0:pp, 0:cols], ACT.Copy, scale=SW).then_inc(s["w_hi"], 1)

            def tile_part(it, tile, rk, jobs):
                for i, st, k in stages(0):
                    if rk:
                        tanh_of(it, tile, i + 1, q[(k + 1) % STAGES])
                        if k == STAGES - 1:
                            act.activation(qp[tile % 2][:, 0, :, st * B:(st + 1) * B], q[0][:], ACT.Copy,
                                           scale=SX).then_inc(s["qh_rdy"], 1)
                    if not jobs:
                        continue
                    for j in AT_STAGE[i]:
                        n = (JOBS, tile - 1, j)
                        act.wait_ge(s["up_mm"], at(it, *n) + 1)
                        act.activation(hid[:], ps_g[:, 0:H], ACT.Silu, scale=1.0 / (SW * SX)).then_inc(s["sg_rdy"], 1)
                        if j == 0:
                            act.wait_ge(s["lg_mm"], at(it, 1, tile - 1) + 1)
                            act.activation(r["z"][:], ps_l[:, 0:E], ACT.Copy, scale=1.0 / (SW * SX))
                            act.activation(r["zt"][:], ps_l[:, 0:E], ACT.Silu, scale=1.0 / (SW * SX))
                            act.activation(r["sc"][:], ps_l[:, 0:E], ACT.Tanh,
                                           scale=0.5 / (SW * SX)).then_inc(s["sc_rdy"], 1)
                        act.wait_ge(s["ht_mm"], at(it, *n) + 1)
                        act.activation(ht[:, 0, 0:2], ps_t[:, 0:2], ACT.Copy)
                        act.activation(ht[0:96, 0, 2], ps_t[0:96, 2], ACT.Copy).then_inc(s["hth_rdy"], 1)

            tile_part(None, 0, True, False)
            with act.Fori(0, TILES // 2 - 1) as it:
                for h in range(2):
                    tile_part(it, 1 + h, True, True)
            tile_part(None, TILES - 1, True, True)
            tile_part(None, TILES, False, True)

        @block.vector
        def _(dve):
            stt = dve.scalar_tensor_tensor
            dve.wait_ge(s["cond_in"], 16)
            dve.tensor_scalar(p[0][:], q[0][:], -SHIFT, None, ALU.add).then_inc(s["p_rdy"], 1)
            dve.tensor_scalar(q[0][:], q[0][:], 1.0, None, ALU.mult).then_inc(s["q_rdy"], 1)
            dve.wait_ge(s["th_rdy"], 1)
            stt(th[:, 1], tanh[:], ST, th[:, 0], ALU.mult, ALU.subtract).then_inc(s["tl_rdy"], 1)
            for n, (_, pp, cols, hi, lo) in enumerate(pieces):
                dve.wait_ge(s["w_hi"], n + 1)
                stt(lo, stage_buf[n % 2][0:pp, 0:cols], SW, hi, ALU.mult, ALU.subtract).then_inc(s["w_lo"], 1)

            def stage(it, tile, i, st, k):
                g = at(it, GS, tile, i)
                t = at(it, STEPS, tile, st)
                d = drv[st]
                last = k == STAGES - 1
                dve.wait_ge(s["sq_rdy"], g + 1)
                stt(base[:], sq[:], 1.0, q[k][:], ALU.subtract, ALU.mult).then_inc(s["cubic_rdy"], 1)
                if k == 0:
                    dve.wait_ge(s["d_rdy"], t + 1)
                    stt(ref[:], d[:], STEP[0], q[0][:], ALU.mult, ALU.add).then_inc(s["ref_rdy"], 1)
                if k == 2:
                    stt(ref[:], d[:], STEP[2], q[0][:], ALU.mult, ALU.add).then_inc(s["ref_rdy"], 1)
                    stt(q[1][:], q[2][:], 2.0, q[1][:], ALU.mult, ALU.add).then_inc(s["qsum_rdy"], 1)
                if last:
                    dve.tensor_scalar(ref[:], d[:], STEP[3], None, ALU.mult).then_inc(s["d_used"], 1)
                    dve.wait_ge(s["qsum_rdy"], 3 * t + 2)
                    dve.tensor_tensor(q[1][:], q[1][:], q[3][:], ALU.add).then_inc(s["qsum_rdy"], 1)
                dve.wait_ge(s["cubic_rdy"], g + 1)
                dve.wait_ge(s["p_rdy"], g + 1)
                dve.tensor_tensor(base[:], base[:], p[k][:], ALU.add).then_inc(s["slope_rdy"], 1)
                if k == 2:
                    dve.wait_ge(s["qsum_rdy"], 3 * t + 1)
                    dve.tensor_tensor(q[1][:], q[1][:], q[0][:], ALU.subtract).then_inc(s["qsum_rdy"], 1)
                if last:
                    dve.wait_ge(s["qsum_rdy"], 3 * t + 3)
                    dve.wait_ge(s["d_used"], t + 1)
                    stt(ref[:], q[1][:], 1.0 / 3.0, ref[:], ALU.mult, ALU.add).then_inc(s["ref_rdy"], 1)
                dve.wait_ge(s["slope_rdy"], g + 1)
                dve.wait_ge(s["ref_rdy"], 3 * t + {0: 1, 1: 1, 2: 2, 3: 3}[k])
                stt(base[:], base[:], -STEP[k], ref[:], ALU.mult, ALU.add).then_inc(s["base_rdy"], 1)
                dve.wait_ge(s["base_rdy"], g + 1)
                dve.wait_ge(s["rk_mm"], g + 1)
                if last:
                    stt(base[:], ps_rk[:], STEP[k] / (SW * ST), base[:], ALU.mult, ALU.add).then_inc(s["next_raw"], 1)
                else:
                    stt(q[k + 1][:], ps_rk[:], STEP[k] / (SW * ST), base[:], ALU.mult, ALU.add).then_inc(s["q_rdy"], 1)
                stt(vel[:], p[k][:], -BETA, q[k][:], ALU.mult, ALU.add).then_inc(s["v_rdy"], 1)
                if last:
                    dve.wait_ge(s["next_raw"], t + 1)
                    dve.tensor_scalar(q[0][:], base[:], -CLAMP, CLAMP, ALU.max, ALU.min).then_inc(s["q_rdy"], 1)
                if not last:
                    dve.wait_ge(s["v_rdy"], g + 1)
                    stt(p[k + 1][:], vel[:], STEP[k] * EPS, p[0][:], ALU.mult, ALU.add).then_inc(s["p_rdy"], 1)
                    if k == 1:
                        dve.wait_ge(s["p_rdy"], g + 2)
                        stt(p[1][:], p[2][:], 2.0, p[1][:], ALU.mult, ALU.add).then_inc(s["psum_rdy"], 1)
                    if k == 2:
                        dve.wait_ge(s["p_rdy"], g + 2)
                        dve.wait_ge(s["psum_rdy"], 4 * t + 1)
                        dve.tensor_tensor(p[1][:], p[1][:], p[3][:], ALU.add).then_inc(s["psum_rdy"], 1)
                else:
                    dve.wait_ge(s["psum_rdy"], 4 * t + 2)
                    dve.tensor_tensor(p[1][:], p[1][:], p[0][:], ALU.subtract).then_inc(s["psum_rdy"], 1)
                    dve.wait_ge(s["v_rdy"], g + 1)
                    dve.tensor_scalar(vel[:], vel[:], STEP[3] * EPS, None, ALU.mult).then_inc(s["v_rdy2"], 1)
                    dve.wait_ge(s["v_rdy2"], t + 1)
                    dve.wait_ge(s["psum_rdy"], 4 * t + 3)
                    stt(p[1][:], p[1][:], 1.0 / 3.0, vel[:], ALU.mult, ALU.add).then_inc(s["psum_rdy"], 1)
                    dve.wait_ge(s["psum_rdy"], 4 * t + 4)
                    dve.tensor_scalar(p[0][:], p[1][:], -CLAMP - SHIFT, CLAMP - SHIFT, ALU.max,
                                      ALU.min).then_inc(s["p_rdy"], 1)
                dve.wait_ge(s["th_rdy"], g + 2)
                stt(th[:, 1], tanh[:], ST, th[:, 0], ALU.mult, ALU.subtract).then_inc(s["tl_rdy"], 1)
                if last:
                    dve.wait_ge(s["qh_rdy"], t + 1)
                    cols = slice(st * B, (st + 1) * B)
                    stt(qp[tile % 2][:, 1, :, cols], q[0][:], SX, qp[tile % 2][:, 0, :, cols], ALU.mult,
                        ALU.subtract).then_inc(s["qp_rdy"], 1)

            def routing(it, tile):
                c = [0]
                R = 21

                def step(ins):
                    c[0] += 1
                    ins.then_inc(s["route"], 1)
                    dve.wait_ge(s["route"], at(it, R, tile, c[0]))

                dve.wait_ge(s["sc_rdy"], at(it, 1, tile) + 1)
                step(dve.tensor_scalar(r["lo"][:], r["z"][:], -1.0, None, ALU.min))
                step(dve.reciprocal(r["lo"][:], r["lo"][:]))
                step(dve.tensor_tensor(r["lo"][:], r["zt"][:], r["lo"][:], ALU.mult))
                step(stt(r["lo"][:], r["z"][:], -1.0, r["lo"][:], ALU.is_lt, ALU.mult))
                step(dve.tensor_scalar(r["sc"][:], r["sc"][:], 0.5, 0.5, ALU.mult, ALU.add))
                step(stt(r["sc"][:], r["z"][:], -1.0, r["sc"][:], ALU.is_ge, ALU.mult))
                step(dve.tensor_tensor(r["sc"][:], r["sc"][:], r["lo"][:], ALU.add))
                step(dve.tensor_tensor(r["sel"][:], r["sc"][:], gb[:], ALU.add))
                for a in (1, 2):
                    mx, key, idx, one = m[f"m{a}"], r[f"k{a}"], m[f"i{a}"], r[f"o{a}"]
                    step(dve.tensor_reduce(mx[:], r["sel"][:], AXIS.X, ALU.max))
                    step(stt(key[:], r["sel"][:], mx[:], desc[:], ALU.is_equal, ALU.mult))
                    step(dve.tensor_reduce(idx[:], key[:], AXIS.X, ALU.max))
                    step(dve.tensor_scalar(one[:], desc[:], idx[:], None, ALU.is_equal))
                    if a == 1:
                        step(stt(r["sel"][:], one[:], -1e30, r["sel"][:], ALU.mult, ALU.add))
                step(dve.tensor_tensor(r["o1"][:], r["o1"][:], r["o2"][:], ALU.add))
                step(dve.tensor_tensor(r["o1"][:], r["o1"][:], r["sc"][:], ALU.mult))
                step(dve.tensor_reduce(m["den"][:], r["o1"][:], AXIS.X, ALU.add))
                step(dve.reciprocal(m["rd"][:], m["den"][:]))
                assert c[0] == R
                dve.tensor_scalar(r["wt"][:], r["o1"][:], m["rd"][:], 1.0 / (SW * SH), ALU.mult,
                                  ALU.mult).then_inc(s["route_rdy"], 1)

            def evacuate(it, tile, j):
                par = tile % 2
                dve.wait_ge(s["y_mm"], at(it, JOBS, tile, j) + 1)
                if j == 0:
                    dve.wait_ge(s[f"acc_in{par}"], at(it, 8, tile - par) + 16)
                if j == 2:
                    dve.wait_ge(s["route_rdy"], at(it, 1, tile) + 1)
                scale = 1.0 / (SW * SH) if j < 2 else r["wt"][:, ORDER[j]:ORDER[j] + 1]
                if j:
                    dve.wait_ge(s["y_done"], at(it, JOBS, tile, j))
                stt(acc[par][:], ps_y[:], scale, acc[par][:], ALU.mult, ALU.add).then_inc(s["y_done"], 1)

            def tile_part(it, tile, rk, jobs, first=False):
                for i, st, k in stages(0):
                    if rk:
                        stage(it, tile, i, st, k)
                    if not jobs:
                        continue
                    for j in AT_STAGE[i]:
                        n = (JOBS, tile - 1, j)
                        dve.wait_ge(s["sg_rdy"], at(it, *n) + 1)
                        stt(hid[:], ps_u[:, 0:H], SH / (SW * SX), hid[:], ALU.mult, ALU.mult).then_inc(s["h_rdy"], 1)
                        if j == 0:
                            routing(it, tile - 1)
                        else:
                            evacuate(it, tile - 1, j - 1)
                        dve.wait_ge(s["hth_rdy"], at(it, *n) + 1)
                        dve.tensor_tensor(ht[:, 1, 0:2], ps_t[:, 0:2], ht[:, 0, 0:2], ALU.subtract)
                        dve.tensor_tensor(ht[0:96, 1, 2], ps_t[0:96, 2], ht[0:96, 0, 2],
                                          ALU.subtract).then_inc(s["hts_rdy"], 1)
                if jobs:
                    evacuate(it, tile - 1, JOBS - 1)

            tile_part(None, 0, True, False)
            with dve.Fori(0, TILES // 2 - 1) as it:
                for h in range(2):
                    tile_part(it, 1 + h, True, True)
            tile_part(None, TILES - 1, True, True)
            tile_part(None, TILES, False, True)

        @block.tensor
        def _(pe):
            mm = pe.matmul

            def chain(it, tile, i):
                pe.wait_ge(s["tl_rdy"], at(it, GS, tile, i) + 1)
                for o in range(NC):
                    for k in range(NC):
                        hi, lo = (cw[:, a, k, o * P:(o + 1) * P] for a in range(2))
                        mm(ps_rk[:, o], hi, th[:, 0, k], start=k == 0, stop=False)
                        mm(ps_rk[:, o], hi, th[:, 1, k], start=False, stop=False)
                        last = mm(ps_rk[:, o], lo, th[:, 0, k], start=False, stop=k == NC - 1)
                last.then_inc(s["rk_mm"], 1)

            def router(it, tile):
                x = qp[tile % 2]
                for k in range(NC):
                    mm(ps_l[:, 0:E], x[:, 0, k], gw[:, 0, k], start=k == 0, stop=False)
                    mm(ps_l[:, 0:E], x[:, 0, k], gw[:, 1, k], start=False, stop=False)
                    last = mm(ps_l[:, 0:E], x[:, 1, k], gw[:, 0, k], start=False, stop=k == NC - 1)
                last.then_inc(s["lg_mm"], 1)

            def up_of(it, tile, j):
                x, e = qp[tile % 2], ORDER[j]
                if j == 0:
                    pe.wait_ge(s["qp_rdy"], at(it, STEPS, tile) + STEPS)
                    router(it, tile)
                for k in range(NC):
                    for a, b in ((0, 0), (0, 1), (1, 0)):
                        for half, ps in enumerate((ps_g, ps_u)):
                            c = k * UPC + half * H
                            last = mm(ps[:, 0:H], x[:, a, k], w[:, e, b, c:c + H],
                                      start=k == 0 and a == b, stop=k == NC - 1 and a == 1)
                last.then_inc(s["up_mm"], 1)

            def down_of(it, tile, j):
                e = ORDER[j]
                pe.wait_ge(s["hts_rdy"], at(it, JOBS, tile, j) + 1)
                for k, (_, hn) in enumerate(HK):
                    for a, b in ((0, 0), (0, 1), (1, 0)):
                        c = UP + k * N
                        last = mm(ps_y[:], ht[0:hn, a, k], w[0:hn, e, b, c:c + N],
                                  start=k == 0 and a == b, stop=k == len(HK) - 1 and a == 1)
                last.then_inc(s["y_mm"], 1)

            def turn_of(it, tile, j):
                pe.wait_ge(s["h_rdy"], at(it, JOBS, tile, j) + 1)
                for k, (h0, hn) in enumerate(HK):
                    last = pe.transpose(ps_t[0:hn, k], hid[:, h0:h0 + hn], ident[:])
                last.then_inc(s["ht_mm"], 1)

            def tile_part(it, tile, rk, jobs):
                for i in range(GS):
                    if rk:
                        chain(it, tile, i)
                    if not jobs:
                        continue
                    for j in AT_STAGE[i]:
                        up_of(it, tile - 1, j)
                        if j:
                            down_of(it, tile - 1, j - 1)
                        turn_of(it, tile - 1, j)
                if jobs:
                    down_of(it, tile - 1, JOBS - 1)

            pe.wait_ge(s["ident_rdy"], 2 + E)
            pe.wait_ge(s["w_lo"], NP)
            tile_part(None, 0, True, False)
            with pe.Fori(0, TILES // 2 - 1) as it:
                for h in range(2):
                    tile_part(it, 1 + h, True, True)
            tile_part(None, TILES - 1, True, True)
            tile_part(None, TILES, False, True)


def kernel(x, cond_2048, L0_cond_coupling, L0_cond_bias, L0_ffn_gate_w, L0_ffn_gate_bias, L0_ffn_shared_gw,
           L0_ffn_shared_dw, L0_ffn_up_w, L0_ffn_down_w):
    import concourse.bacc as _bacc
    from concourse.bass_utils import run_bass_kernel_spmd as _run

    def split(a, n):
        return np.ascontiguousarray(a.reshape(n, P, -1).transpose(1, 0, 2))

    x, cond_2048 = np.asarray(x), np.asarray(cond_2048)
    xt = x.transpose(1, 0, 2)
    sg, sd = np.asarray(L0_ffn_shared_gw), np.asarray(L0_ffn_shared_dw)
    ups = [np.asarray(u) for u in np.asarray(L0_ffn_up_w)]
    downs = [np.asarray(d) for d in np.asarray(L0_ffn_down_w)]
    for i in range(2):
        part = slice(i * H, (i + 1) * H)
        ups.append(np.concatenate([sg[2 * H:][part], sg[:2 * H][part]]))
        downs.append(sd[:, part])
    arrays = {
        "in_drive": np.ascontiguousarray(xt.reshape(T, B, NC, P).transpose(0, 3, 2, 1)),
        "in_cond": np.ascontiguousarray(cond_2048.reshape(B, NC, P).transpose(2, 1, 0)),
        "in_rows": np.ascontiguousarray(xt.reshape(T * B, N)),
        "in_coupling": split(np.asarray(L0_cond_coupling).T, NC),
        "in_bias": np.ascontiguousarray(np.asarray(L0_cond_bias).reshape(NC, P).T),
        "in_gate": split(np.asarray(L0_ffn_gate_w).T, NC).reshape(P, NC * E),
        "in_gate_bias": np.ascontiguousarray(np.asarray(L0_ffn_gate_bias)),
        "in_up": np.stack([split(u.T, NC).reshape(P, UP) for u in ups]),
        "in_down": np.stack([np.ascontiguousarray(d.T) for d in downs]),
    }
    nc = _bacc.Bacc("TRN2", target_bir_lowering=False, num_devices=1)
    aps = [nc.dram_tensor(n, a.shape, F32, kind="ExternalInput").ap() for n, a in arrays.items()]
    out = nc.dram_tensor("result", (T * B, N), F32, kind="ExternalOutput").ap()
    build(nc, *aps, out)
    r = _run(nc, [arrays], core_ids=[0])
    return np.ascontiguousarray(r.results[0]["result"].reshape(T, B, N).transpose(1, 0, 2))
```

```python
from contextlib import ExitStack

import numpy as np

import concourse.bass as bass
from concourse import mybir

F32 = mybir.dt.float32
F16 = mybir.dt.float16
I32 = mybir.dt.int32
ACT = mybir.ActivationFunctionType
ALU = mybir.AluOpType
AXIS = mybir.AxisListType

P = 128
B, T, N = 64, 64, 512
NC = N // P
E = 8
H = 352
TOKENS = B * T
TILES = TOKENS // P
STEPS = P // B
STAGES = 4
GS = STEPS * STAGES
UP = NC * 2 * H
HK = [(k, min(P, H - k)) for k in range(0, H, P)]
WC = UP + len(HK) * N

DT, EPS, ALPHA, BETA, CLAMP = 0.01, 0.08, 0.7, 0.8, 20.0
STEP = [DT / 2, DT / 2, DT, DT / 6]

SW = 2.0 ** 8
SX = 2.0 ** 11
ST = 2.0 ** 15
SH = 2.0 ** 4

ROW = N + 1 + E
REGION = TOKENS + P
NO_ROWS = E * REGION
SLOTS = (TOKENS * 2 + E * (P - 1)) // P + 1
LAG = 5
XFIRST = 2 * (TILES - LAG)

PIECES = [(c, min(N, UP - c), P) for c in range(0, UP, N)] + [(UP + k * N, N, HK[k][1]) for k in range(len(HK))]
PT = 2 * len(PIECES)
FIRST = NC + 1
WTILES = (E + 2) // 2
STG = 3
PIECES_AT = [range(i * PT // GS, (i + 1) * PT // GS) for i in range(GS)]
assert PT % STG == 0
ROUTE_AT = [((), (), ()), ((), (0,), (1, 2, 3, 4, 5)), ((6,), (7,), (8, 9, 10, 11, 12)), ((13,), (14,), ()),
            ((15,), (16,), (17, 18, 19, 20, 21)), ((), (), (22, 23, 24, 25, 26, 27)),
            ((28,), (29,), (30, 31, 32, 33, 34, 35)), ((36,), (37,), (38, 39))]
NROUTE, ENTER = 40, 29


class Pos:

    def __init__(self, tile, jobs=0, xjobs=0, jpt=0, xpt=0, it=None):
        self.tile, self.jobs0, self.x0, self.jpt, self.xpt, self.it = tile, jobs, xjobs, jpt, xpt, it

    def _at(self, per, base):
        return base if self.it is None or per == 0 else self.it * per + base

    def tiles(self, per, off=0, local=0):
        return self._at(per, per * (self.tile + off) + local)

    def jobs(self, j):
        return self._at(self.jpt, self.jobs0 + j)

    def pairs(self, x, per, local=0):
        return self._at(per * self.xpt // 2, per * ((self.x0 + x) // 2) + local)

    def xjobs(self, x, per=1, local=0):
        return self._at(self.xpt * per, per * (self.x0 + x) + local)


START = Pos(0)
FIRSTS = Pos(1)
TAKING = dict(tile=2, jobs=2, jpt=2)
BEFORE = Pos(WTILES, jobs=2 * (WTILES - 1))
FIRSTX = Pos(LAG + 1, jobs=2 * LAG)
MAIN = dict(tile=LAG + 2, jobs=2 * LAG + 4, xjobs=2, jpt=4, xpt=2)
NMAIN = TILES - LAG - 2
MAINEND = Pos(TILES - 1, jobs=2 * LAG + 4 * NMAIN, xjobs=2 * NMAIN)
ENDING = Pos(TILES, jobs=2 * LAG + 4 * (TILES - LAG - 1), xjobs=XFIRST - 2)
TAIL = dict(tile=TILES + 1, jobs=2 * LAG + 4 * (TILES - LAG), xjobs=XFIRST, jpt=2, xpt=2)
REST = dict(TAIL, jobs=TAIL["jobs"] + 2, xjobs=TAIL["xjobs"] + 2)
NTAIL = (SLOTS - XFIRST) // 2
LASTS = Pos(TILES + 1, jobs=TAIL["jobs"] + 2 * (NTAIL - 1), xjobs=SLOTS - 2)
assert WTILES == LAG and SLOTS % 2 == 0


def build(nc, drive, cond, rows, coupling, bias, gate, gate_bias, up, down, out, xs):
    with ExitStack() as ctx:
        def sb(name, shape, dt=F32):
            return ctx.enter_context(nc.sbuf_tensor(name, shape, dt))

        def pb(name, shape, dt=F32):
            return ctx.enter_context(nc.psum_tensor(name, shape, dt))

        w = sb("w", [P, E + 2, 2, WC], F16)
        cw = sb("cw", [P, 2, NC, N], F16)
        gw = sb("gw", [P, 2, NC, E], F16)
        gb = sb("gb", [P, E])
        bias_sb = sb("bias_sb", [P, NC])
        q = [sb(f"q{i}", [P, NC, B]) for i in range(3)]
        p = [sb(f"p{i}", [P, NC, B]) for i in range(3)]
        q, p = q + [q[2]], p + [p[2]]
        base = sb("base", [P, NC, B])
        vel = sb("vel", [P, NC, B])
        ref = sb("ref", [P, NC, B])
        th = sb("th", [P, 2, NC, B], F16)
        drv = [sb(f"drv{i}", [P, NC, B]) for i in range(STEPS)]
        qp = sb("qp", [P, 2, NC, P], F16)
        hid = sb("hid", [P, H])
        ht = sb("ht", [P, 2, len(HK), P], F16)
        io = sb("io", [P, ROW])
        x_in = sb("x_in", [P, N])
        res = sb("res", [P, N])
        x_t = sb("x_t", [P, 2, NC, P], F16)
        y = sb("y", [P, N])
        ident = sb("ident", [P, P])
        ident16 = sb("ident16", [P, P], F16)
        upper = sb("upper", [P, P], F16)
        ones = sb("ones", [P, P], F16)
        desc = sb("desc", [P, E])
        r = {k: sb("r_" + k, [P, E]) for k in "sc z zt lo key o1 o2".split()}
        chosen = sb("chosen", [P, E], F16)
        pre = [sb(f"pre{i}", [P, E + 4]) for i in range(3)]
        count = sb("count", [P, E])
        rem = sb("rem", [P, E])
        code = sb("code", [P, E])
        eidx = sb("eidx", [P, E])
        cols = sb("cols", [P, 11])
        mx, ix, part, slots_of, filled = (cols[:, c:c + 1] for c in range(5))
        lst, lv = cols[:, 5:7], cols[:, 7:9]
        idx = sb("idx", [P, 2], I32)
        fill_idx = r["o1"][:].bitcast(I32)
        todo = sb("todo", [1, 2 * SLOTS], I32)
        tok = [sb(f"tok{i}", [P, 1], I32) for i in range(2)]
        ws = [cols[:, 9 + i:10 + i] for i in range(2)]

        ps_rk = pb("ps_rk", [P, NC, B])
        ps_g = pb("ps_g", [P, 512])
        ps_u = pb("ps_u", [P, 512])
        ps_t = pb("ps_t", [P, len(HK), P])
        ps_y = pb("ps_y", [P, N])
        ps_l = pb("ps_l", [P, 512])
        ps_x = pb("ps_x", [P, 2 * NC, P], F16)
        tanh = pb("tanh", [P, 2, NC, B])[:, 0]
        LOGIT, RANK, TOTAL, LIST = slice(0, E), slice(16, 16 + E), slice(32, 32 + E), 64

        names = ("blank cond_in consts_in consts set_up zeroed bias_rdy "
                 "w_in0 w_in1 w_in2 w_hi w_lo "
                 "tanh_rdy th_rdy tl_rdy sq_rdy rk_mm cubic_rdy base_rdy next_raw q_rdy "
                 "v_rdy w_rdy p_rdy p0_rdy half_base ref_rdy ref2_rdy z_rdy third_rdy drv_in0 drv_in1 d_rdy "
                 "qsum psum1 psum3 psum3a psum4 qh_rdy qp_rdy "
                 "up_mm sg_rdy h_rdy ht_mm hth_rdy hts_rdy y_mm lg_mm sc_rdy route "
                 "chosen_rdy rank_mm idx_rdy list_rdy list_mm todo_rdy "
                 "rows_mm rows_rdy tags_rdy sending sent1 sent2 stored res_in res_rdy "
                 "x_in_rdy xt_mm x_t_rdy tag_in0 tag_in1 y_rdy y_free fill_rdy fill_in filled_up").split()
        s = {n: ctx.enter_context(nc.semaphore(n)) for n in names}
        stage_buf = [x_in[:], y[:], x_t[:].rearrange("p a b c -> p (a b c)").bitcast(F32)]

        def p_ready(eng, pos, i):
            k, st = i % STAGES, i // STAGES
            if k == 0:
                eng.wait_ge(s["p0_rdy"], pos.tiles(STEPS, 0, st + 1))
            else:
                eng.wait_ge(s["p_rdy"], pos.tiles(3 * STEPS, 0, 3 * st + k))

        def piece(pos, n):
            which, (c, cols, pp) = n // len(PIECES), PIECES[n % len(PIECES)]
            if pos.it is None:
                e = which + (2 * (pos.tile - 1) if pos.tile else E)
                h0 = HK[(c - UP) // N][0] if c >= UP else 0
                src = up[e, :, c:c + cols] if c < UP else down[e, h0:h0 + pp, :]
                return src, pp, cols, w[0:pp, e, 0, c:c + cols], w[0:pp, e, 1, c:c + cols]
            e = pos.it * 2 + (2 * (pos.tile - 1) + which)
            if c < UP:
                src = up[bass.ds(e, 1), :, c:c + cols].rearrange("o p c -> (o p) c")
            else:
                h0 = HK[(c - UP) // N][0]
                src = down[bass.ds(e, 1), h0:h0 + pp, :].rearrange("o p c -> (o p) c")
            hi, lo = (w[0:pp, bass.ds(e, 1), a, c:c + cols].rearrange("p o c -> p (o c)") for a in range(2))
            return src, pp, cols, hi, lo

        def piece_load(eng, pos, n):
            src, pp, cols, _, _ = piece(pos, n)
            b = (FIRST + n) % STG
            eng.wait_ge(s["w_lo"], pos.tiles(PT, 0, FIRST + n - STG + 1))
            eng.dma_start(stage_buf[b][0:pp, 0:cols], src).then_inc(s[f"w_in{b}"], 16)

        def piece_hi(eng, pos, n):
            _, pp, cols, hi, _ = piece(pos, n)
            b = (FIRST + n) % STG
            eng.wait_ge(s[f"w_in{b}"], pos.tiles(PT // STG * 16, 0, 16 * ((FIRST + n) // STG + 1)))
            eng.activation(hi, stage_buf[b][0:pp, 0:cols], ACT.Copy, scale=SW).then_inc(s["w_hi"], 1)

        def piece_lo(eng, pos, n):
            _, pp, cols, hi, lo = piece(pos, n)
            b = (FIRST + n) % STG
            eng.wait_ge(s["w_hi"], pos.tiles(PT, 0, FIRST + n + 1))
            eng.scalar_tensor_tensor(lo, stage_buf[b][0:pp, 0:cols], SW, hi, ALU.mult,
                                     ALU.subtract).then_inc(s["w_lo"], 1)

        first_pieces = [(coupling[:, k, :], N, cw[:, 0, k, :], cw[:, 1, k, :]) for k in range(NC)]
        first_pieces.append((gate, NC * E, gw[:, 0].rearrange("p a b -> p (a b)"), gw[:, 1].rearrange("p a b -> p (a b)")))

        block = ctx.enter_context(nc.Block())

        @block.sync
        def _(sp):
            sp.dma_start(q[0][:], cond).then_inc(s["cond_in"], 16)
            sp.dma_start(bias_sb[:], bias).then_inc(s["consts_in"], 16)
            sp.dma_start(gb[:], gate_bias.rearrange("(a n) -> a n", a=1).to_broadcast([P, E])).then_inc(s["consts_in"], 16)
            for n, (src, cols, _, _) in enumerate(first_pieces):
                b = n % STG
                if n == 1:
                    sp.wait_ge(s["zeroed"], 1)
                    sp.dma_start(out[TOKENS:TOKENS + P, :], y[:]).then_inc(s["blank"], 16)
                    sp.wait_ge(s["blank"], 16)
                if n >= STG:
                    sp.wait_ge(s["w_lo"], n - STG + 1)
                sp.dma_start(stage_buf[b][:, 0:cols], src).then_inc(s[f"w_in{b}"], 16)
            for t in range(STEPS):
                sp.dma_start(drv[t][:], drive[t]).then_inc(s[f"drv_in{t}"], 16)
            sp.wait_ge(s["set_up"], 1)
            sp.dma_start(xs[NO_ROWS:NO_ROWS + P, :], io[:]).then_inc(s["stored"], 16)

            def drive_in(pos, st):
                t = pos.tiles(STEPS, 0, st + STEPS)
                src = drive[t] if pos.it is None else drive[bass.ds(t, 1)].rearrange("o p c b -> (o p) c b")
                sp.wait_ge(s["qsum"], pos.tiles(3 * STEPS, 0, 3 * st + 2))
                sp.dma_start(drv[st][:], src).then_inc(s[f"drv_in{st}"], 16)

            def expert_rows_in(pos, x, row):
                if pos.it is not None or pos.x0 + x > 0:
                    sp.wait_ge(s["xt_mm"], pos.xjobs(x, 1, 0))
                sp.dma_start(x_in[:], xs[bass.ds(row, P), 0:N]).then_inc(s["x_in_rdy"], 16)

            def expert_tags_in(pos, x, row, e):
                if pos.it is not None or pos.x0 + x >= 2:
                    sp.wait_ge(s["y_free"], pos.xjobs(x, 16, -16))
                tag_in = s[f"tag_in{x % 2}"]
                sp.dma_start(tok[x % 2][:].bitcast(F32), xs[bass.ds(row, P), N:N + 1],
                             allow_slow_non_contiguous=True).then_inc(tag_in, 16)
                sp.dma_start(ws[x % 2], xs[bass.ds(row, P), bass.ds(e + (N + 1), 1)],
                             allow_slow_non_contiguous=True).then_inc(tag_in, 16)

            def numbers(pos, x, most, off=0):
                at = pos.xjobs(x, 1, off)
                return sp.value_load(todo[0:1, bass.ds(at, 1)] if pos.it is not None else todo[0:1, at:at + 1],
                                     min_val=0, max_val=most)

            def jobs_of(pos, xs):
                return {x: (numbers(pos, x, NO_ROWS), numbers(pos, x, E - 1, SLOTS)) for x in xs}

            def residual_in(pos):
                r0 = pos.tiles(P, -1)
                src = rows[bass.ds(r0, P), :] if pos.it is not None else rows[r0:r0 + P, :]
                sp.wait_ge(s["stored"], pos.tiles(16))
                sp.dma_start(res[:], src).then_inc(s["res_in"], 16)

            def result_out(pos):
                r0 = pos.tiles(P, -1)
                dst = out[bass.ds(r0, P), :] if pos.it is not None else out[r0:r0 + P, :]
                sp.wait_ge(s["res_rdy"], pos.tiles(1))
                sp.dma_start(dst, res[:]).then_inc(s["stored"], 16)

            def tile_part(pos, chain, weights, ffn, experts):
                if experts:
                    sp.wait_ge(s["todo_rdy"], pos.tiles(1, -1))
                    job = jobs_of(pos, range(2))
                    sp.wait_ge(s["sent1"], pos.tiles(16, -1))
                    sp.wait_ge(s["sent2"], pos.tiles(16, -1))
                    expert_rows_in(pos, 0, job[0][0])
                for i in range(GS):
                    if weights:
                        for n in PIECES_AT[i]:
                            piece_load(sp, pos, n)
                    if ffn and i == 1:
                        residual_in(pos)
                    if chain and i == 3:
                        drive_in(pos, 0)
                    if experts and i == 3:
                        expert_rows_in(pos, 1, job[1][0])
                        expert_tags_in(pos, 0, *job[0])
                    if ffn and i == 6:
                        result_out(pos)
                    if chain and i == 7:
                        drive_in(pos, 1)
                    if experts and i == 7:
                        expert_tags_in(pos, 1, *job[1])

            tile_part(START, True, True, False, False)
            tile_part(FIRSTS, True, True, True, False)
            with sp.Fori(0, WTILES - 2) as it:
                tile_part(Pos(it=it, **TAKING), True, True, True, False)
            tile_part(BEFORE, True, False, True, False)
            sp.wait_ge(s["w_lo"], FIRST + WTILES * PT)
            tile_part(FIRSTX, True, False, True, True)
            with sp.Fori(0, NMAIN - 1) as it:
                tile_part(Pos(it=it, **MAIN), True, False, True, True)
            last = dict(MAIN, tile=MAIN["tile"] + NMAIN - 1, jobs=MAIN["jobs"] + 4 * (NMAIN - 1),
                        xjobs=MAIN["xjobs"] + 2 * (NMAIN - 1))
            tile_part(Pos(**last), False, False, True, True)
            tile_part(ENDING, False, False, True, True)
            sp.wait_ge(s["todo_rdy"], TILES)
            pos = Pos(**TAIL)
            job = jobs_of(pos, range(2))
            sp.wait_ge(s["sent1"], 16 * TILES)
            sp.wait_ge(s["sent2"], 16 * TILES)
            expert_rows_in(pos, 0, job[0][0])
            sp.dma_start(io[:], xs[NO_ROWS:NO_ROWS + P, :]).then_inc(s["fill_in"], 16)
            expert_rows_in(pos, 1, job[1][0])
            expert_tags_in(pos, 0, *job[0])
            sp.wait_ge(s["filled_up"], 16 * E)
            sp.wait_ge(s["todo_rdy"], TILES + 1)
            with sp.Fori(0, NTAIL - 1) as it:
                pos = Pos(it=it, **REST)
                job = jobs_of(pos, range(-1, 2))
                for x in range(2):
                    expert_rows_in(pos, x, job[x][0])
                    expert_tags_in(pos, x - 1, *job[x - 1])
            end = Pos(0, xjobs=SLOTS)
            expert_tags_in(end, -1, *jobs_of(end, [-1])[-1])
            sp.wait_ge(s["y_free"], 16 * SLOTS)

        @block.gpsimd
        def _(pool):
            tt = pool.tensor_tensor
            pool.memset(y[:], 0.0).then_inc(s["zeroed"], 1)
            pool.memset(ident[:], 0.0)
            pool.memset(ident16[:], 0.0)
            pool.memset(ones[:], 1.0)
            pool.memset(upper[:], 1.0).then_inc(s["consts"], 1)
            pool.wait_ge(s["consts"], 1)
            for mat in (ident, ident16):
                pool.affine_select(out=mat[:], in_=mat[:], compare_op=ALU.not_equal, fill=1.0, base=0,
                                   pattern=[[-1, P]], channel_multiplier=1)
            pool.affine_select(out=upper[:], in_=upper[:], compare_op=ALU.is_gt, fill=0.0, base=0,
                               pattern=[[1, P]], channel_multiplier=-1)
            pool.iota(idx[:, 0:1], pattern=[[0, 1]], base=0, channel_multiplier=1)
            pool.memset(io[:], 0.0)
            for e in range(E):
                pool.memset(desc[:, e:e + 1], float(E - e))
                pool.memset(eidx[:, e:e + 1], float(e))
                pool.memset(count[:, e:e + 1], float(e * REGION))
                pool.memset(code[:, e:e + 1], float(e * REGION - NO_ROWS))
            for t in (rem[:], filled, lst[:, 1:2], *(t[:] for t in pre)):
                pool.memset(t, 0.0)
            pool.memset(lst[:, 0:1], float(NO_ROWS)).then_inc(s["consts"], 1)
            pool.wait_ge(s["consts"], 2)
            pool.tensor_copy(slots_of, idx[:, 0:1])
            pool.tensor_copy(part, idx[:, 0:1]).then_inc(s["consts"], 1)
            pool.wait_ge(s["consts"], 3)
            pool.tensor_scalar(io[:, N:N + 1].bitcast(I32), part, float(TOKENS), None, ALU.add).then_inc(s["set_up"], 1)

            def stage(pos, i):
                k, st = i % STAGES, i // STAGES
                g, t = pos.tiles(GS, 0, i), pos.tiles(STEPS, 0, st)
                pool.wait_ge(s["q_rdy"], g + 1)
                if k == 0:
                    pool.wait_ge(s["d_rdy"], t + 1)
                    tt(ref[:], q[0][:], drv[st][:], ALU.add).then_inc(s["ref_rdy"], 1)
                p_ready(pool, pos, i)
                tt(vel[:], q[k][:], p[k][:], ALU.subtract).then_inc(s["v_rdy"], 1)
                if k == 2:
                    pool.wait_ge(s["psum1"], t + 1)
                    pool.wait_ge(s["base_rdy"], g + 1)
                if k == 3:
                    tt(p[1][:], p[1][:], p[3][:], ALU.add).then_inc(s["psum3a"], 1)
                    pool.wait_ge(s["psum3a"], t + 1)
                    tt(p[1][:], p[1][:], p[0][:], ALU.subtract).then_inc(s["psum3"], 1)
                else:
                    pool.wait_ge(s["w_rdy"], g + 1)
                    tt(p[k + 1][:], p[0][:], vel[:], ALU.add).then_inc(s["p_rdy"], 1)
                if k == 1:
                    pool.wait_ge(s["half_base"], g + 1)
                    pool.wait_ge(s["ref_rdy"], t + 1)
                    tt(ref[:], ref[:], drv[st][:], ALU.add).then_inc(s["ref2_rdy"], 1)
                    tt(drv[st][:], drv[st][:], q[0][:], ALU.subtract).then_inc(s["z_rdy"], 1)

            def send_rows(pos):
                pool.wait_ge(s["rows_rdy"], pos.tiles(1))
                pool.wait_ge(s["tags_rdy"], pos.tiles(1))
                pool.wait_ge(s["idx_rdy"], pos.tiles(1))
                pool.sem_inc(s["sending"], 1)
                for a in range(2):
                    pool.indirect_dma_start(
                        out=xs[:, :], out_offset=bass.IndirectOffsetOnAxis(ap=idx[:, a:a + 1], axis=0),
                        in_=io[:], in_offset=None).then_inc(s[f"sent{a + 1}"], 16)

            def add_result(pos, x):
                if pos.it is not None or pos.x0 + x > 0:
                    pool.wait_ge(s["y_free"], pos.xjobs(x, 16, 0))
                pool.wait_ge(s["y_rdy"], pos.xjobs(x, 1, 1))
                pool.sem_inc(s["sending"], 1)
                pool.indirect_dma_start(
                    out=out[:, :], out_offset=bass.IndirectOffsetOnAxis(ap=tok[x % 2][:, 0:1], axis=0),
                    in_=y[:], in_offset=None, compute_op=ALU.add).then_inc(s["y_free"], 16)

            def tile_part(pos, chain, ffn, experts, before):
                for i in range(GS):
                    if chain:
                        stage(pos, i)
                    if before and i == 0:
                        pool.wait_ge(s["stored"], pos.tiles(16))
                        add_result(pos, -2)
                    if before and i == 2:
                        add_result(pos, -1)
                    if ffn and i == 5:
                        send_rows(pos)

            tile_part(START, True, False, False, False)
            tile_part(FIRSTS, True, True, False, False)
            with pool.Fori(0, WTILES - 2) as it:
                tile_part(Pos(it=it, **TAKING), True, True, False, False)
            tile_part(BEFORE, True, True, False, False)
            tile_part(FIRSTX, True, True, True, False)
            with pool.Fori(0, NMAIN) as it:
                tile_part(Pos(it=it, **MAIN), True, True, True, True)
            tile_part(ENDING, False, True, True, True)
            pos = Pos(**TAIL)
            pool.wait_ge(s["stored"], 16 * (TILES + 1))
            add_result(pos, -2)
            add_result(pos, -1)
            pool.wait_ge(s["fill_in"], 16)
            pool.wait_ge(s["fill_rdy"], 1)
            for e in range(E):
                pool.indirect_dma_start(
                    out=xs[:, :], out_offset=bass.IndirectOffsetOnAxis(ap=fill_idx[:, e:e + 1], axis=0),
                    in_=io[:], in_offset=None).then_inc(s["filled_up"], 16)
            add_result(pos, 0)
            with pool.Fori(0, NTAIL - 1) as it:
                for x in range(2):
                    add_result(Pos(it=it, **REST), x - 1)
            add_result(Pos(0, xjobs=SLOTS), -1)

        @block.scalar
        def _(act):
            def tanh_of(pos, i):
                g = pos.tiles(GS, 0, i)
                src = q[i % STAGES]
                act.wait_ge(s["q_rdy"], g + 1)
                act.activation(tanh, src[:], ACT.Tanh).then_inc(s["tanh_rdy"], 1)
                act.wait_ge(s["tanh_rdy"], g + 1)
                act.activation(th[:, 0], tanh, ACT.Copy, scale=ST).then_inc(s["th_rdy"], 1)
                act.activation(base[:], src[:], ACT.Square, scale=3.0 ** -0.5).then_inc(s["sq_rdy"], 1)

            def velocity(pos, i):
                g, k = pos.tiles(GS, 0, i), i % STAGES
                act.wait_ge(s["v_rdy"], g + 1)
                act.activation(vel[:], vel[:], ACT.Copy, scale=STEP[k] * EPS * BETA).then_inc(s["w_rdy"], 1)

            def third(pos, st):
                act.wait_ge(s["z_rdy"], pos.tiles(STEPS, 0, st + 1))
                act.activation(drv[st][:], drv[st][:], ACT.Copy, scale=1.0 / 3.0).then_inc(s["third_rdy"], 1)

            tanh_of(START, 0)
            for n, (_, cols, hi, _) in enumerate(first_pieces):
                act.wait_ge(s[f"w_in{n % STG}"], 16 * (n // STG + 1))
                act.activation(hi, stage_buf[n % STG][:, 0:cols], ACT.Copy, scale=SW).then_inc(s["w_hi"], 1)

            def gate_of(pos, j):
                act.wait_ge(s["up_mm"], pos.jobs(j) + 1)
                act.activation(hid[:], ps_g[:, 0:H], ACT.Silu, scale=1.0 / (SW * SX)).then_inc(s["sg_rdy"], 1)

            def hidden_lead(pos, j):
                act.wait_ge(s["ht_mm"], pos.jobs(j) + 1)
                act.activation(ht[:, 0], ps_t[:], ACT.Copy).then_inc(s["hth_rdy"], 1)

            def scores(pos):
                act.wait_ge(s["lg_mm"], pos.tiles(1))
                act.activation(r["z"][:], ps_l[:, LOGIT], ACT.Copy, scale=1.0 / (SW * SX))
                act.activation(r["zt"][:], ps_l[:, LOGIT], ACT.Silu, scale=1.0 / (SW * SX))
                act.activation(r["sc"][:], ps_l[:, LOGIT], ACT.Tanh, scale=0.5 / (SW * SX)).then_inc(s["sc_rdy"], 1)

            def rows_of(pos):
                act.wait_ge(s["rows_mm"], pos.tiles(1))
                if pos.tile > 1:
                    act.wait_ge(s["sent1"], pos.tiles(16, -1))
                    act.wait_ge(s["sent2"], pos.tiles(16, -1))
                act.activation(io[:, 0:N].bitcast(F16), ps_x[:].rearrange("p a b -> p (a b)"),
                               ACT.Copy).then_inc(s["rows_rdy"], 1)

            def expert_x(pos, x):
                act.wait_ge(s["xt_mm"], pos.xjobs(x, 1, 1))
                act.activation(x_t[:].rearrange("p a b c -> p (a b) c"), ps_x[:], ACT.Copy).then_inc(s["x_t_rdy"], 1)

            def weighted(pos, x, j):
                act.wait_ge(s["y_mm"], pos.jobs(j) + 1)
                act.wait_ge(s[f"tag_in{x % 2}"], pos.pairs(x, 32, 32))
                if pos.it is not None or pos.x0 + x > 0:
                    act.wait_ge(s["y_free"], pos.xjobs(x, 16, 0))
                act.activation(y[:], ps_y[:], ACT.Identity, scale=ws[x % 2]).then_inc(s["y_rdy"], 1)

            def tile_part(pos, chain, weights, ffn, experts, before):
                for i in range(GS):
                    if chain and i % STAGES:
                        velocity(pos, i)
                    if before and i == 0:
                        hidden_lead(pos, -1)
                    if ffn and i in (1, 3):
                        gate_of(pos, i // 2)
                    if experts and i in (5, 7):
                        gate_of(pos, i // 2)
                    if ffn and i in (2, 4):
                        hidden_lead(pos, i // 2 - 1)
                    if experts and i == 6:
                        hidden_lead(pos, 2)
                    if chain and i % STAGES == 0:
                        velocity(pos, i)
                    if weights:
                        for n in PIECES_AT[i]:
                            piece_hi(act, pos, n)
                    if chain:
                        tanh_of(pos, i + 1)
                        if i % STAGES == 1:
                            third(pos, i // STAGES)
                        if i % STAGES == STAGES - 1:
                            st = i // STAGES
                            act.activation(qp[:, 0, :, st * B:(st + 1) * B], q[0][:], ACT.Copy,
                                           scale=SX).then_inc(s["qh_rdy"], 1)
                    if ffn and i == 0:
                        scores(pos)
                    if ffn and i == 1:
                        rows_of(pos)
                        if before:
                            weighted(pos, -1, -1)
                    if experts and i == 3:
                        expert_x(pos, 0)
                    if experts and i == 5:
                        expert_x(pos, 1)
                    if experts and i == 7:
                        weighted(pos, 0, 2)

            def tail_part(pos, final=False):
                for x in range(2):
                    gate_of(pos, x)
                    if not (final and x == 1):
                        expert_x(pos, x + 1)
                    weighted(pos, x - 1, x - 1)
                    hidden_lead(pos, x)

            tile_part(START, True, True, False, False, False)
            act.wait_ge(s["stored"], 16)
            tile_part(FIRSTS, True, True, True, False, False)
            with act.Fori(0, WTILES - 2) as it:
                tile_part(Pos(it=it, **TAKING), True, True, True, False, False)
            tile_part(BEFORE, True, False, True, False, False)
            tile_part(FIRSTX, True, False, True, True, False)
            with act.Fori(0, NMAIN) as it:
                tile_part(Pos(it=it, **MAIN), True, False, True, True, True)
            tile_part(ENDING, False, False, True, True, True)
            pos = Pos(**TAIL)
            hidden_lead(pos, -1)
            expert_x(pos, 0)
            tail_part(pos)
            with act.Fori(0, NTAIL - 2) as it:
                tail_part(Pos(it=it, **REST))
            tail_part(LASTS, True)
            weighted(Pos(0, jobs=TAIL["jobs"] + 2 * NTAIL, xjobs=SLOTS), -1, -1)

        @block.vector
        def _(dve):
            stt, tt = dve.scalar_tensor_tensor, dve.tensor_tensor
            dve.memset(ps_t[:], 0.0)
            dve.wait_ge(s["cond_in"], 16)
            dve.tensor_scalar(p[0][:], q[0][:], BETA, -ALPHA, ALU.mult, ALU.add).then_inc(s["p0_rdy"], 1)
            dve.tensor_scalar(q[0][:], q[0][:], 1.0, None, ALU.mult).then_inc(s["q_rdy"], 1)
            dve.wait_ge(s["consts_in"], 32)
            dve.tensor_scalar(bias_sb[:], bias_sb[:], -ALPHA / BETA, DT / 2, ALU.add, ALU.mult).then_inc(s["bias_rdy"], 1)
            dve.wait_ge(s["th_rdy"], 1)
            stt(th[:, 1], tanh, ST, th[:, 0], ALU.mult, ALU.subtract).then_inc(s["tl_rdy"], 1)
            for n, (_, cols, hi, lo) in enumerate(first_pieces):
                dve.wait_ge(s["w_hi"], n + 1)
                stt(lo, stage_buf[n % STG][:, 0:cols], SW, hi, ALU.mult, ALU.subtract).then_inc(s["w_lo"], 1)
            dve.wait_ge(s["bias_rdy"], 1)

            def vars_of(pos):
                return dict(tile=pos.tile, jobs=pos.jobs0, xjobs=pos.x0, jpt=pos.jpt, xpt=pos.xpt, it=pos.it)

            def drive_of(pos, st):
                dve.wait_ge(s[f"drv_in{st}"], pos.tiles(16, 0, 16))
                stt(drv[st][:], drv[st][:], DT / 2, bias_sb[:].rearrange("p (c o) -> p c o", o=1).to_broadcast([P, NC, B]),
                    ALU.mult, ALU.add).then_inc(s["d_rdy"], 1)

            def base_of(pos, i, ffn):
                k, st = i % STAGES, i // STAGES
                g, t = pos.tiles(GS, 0, i), pos.tiles(STEPS, 0, st)
                if k == 3:
                    dve.wait_ge(s["qsum"], 3 * t + 2)
                    stt(q[1][:], q[3][:], 1.0 / 3.0, q[1][:], ALU.mult, ALU.add).then_inc(s["qsum"], 1)
                dve.wait_ge(s["sq_rdy"], g + 1)
                stt(base[:], base[:], 1.0, q[k][:], ALU.subtract, ALU.mult).then_inc(s["cubic_rdy"], 1)
                if i == 0 and ffn:
                    end_of_tile(pos)
                if ffn:
                    routing(pos, ROUTE_AT[i][0])
                if k < 2:
                    dve.wait_ge(s["ref_rdy"], t + 1)
                elif k == 2:
                    dve.wait_ge(s["ref2_rdy"], t + 1)
                else:
                    dve.wait_ge(s["qsum"], 3 * t + 3)
                dve.wait_ge(s["cubic_rdy"], g + 1)
                stt(base[:], base[:], -STEP[k], (q[1] if k == 3 else ref)[:], ALU.mult,
                    ALU.add).then_inc(s["half_base"], 1)
                if ffn:
                    routing(pos, ROUTE_AT[i][1])
                p_ready(dve, pos, i)
                dve.wait_ge(s["half_base"], g + 1)
                stt(base[:], p[k][:], -STEP[k] / BETA, base[:], ALU.mult, ALU.add).then_inc(s["base_rdy"], 1)
                if k == 2:
                    stt(q[1][:], q[2][:], 2.0, q[1][:], ALU.mult, ALU.add).then_inc(s["qsum"], 1)

            def next_state(pos, i):
                k, st = i % STAGES, i // STAGES
                g, t = pos.tiles(GS, 0, i), pos.tiles(STEPS, 0, st)
                if k == 2:
                    dve.wait_ge(s["v_rdy"], g + 1)
                    dve.wait_ge(s["qsum"], 3 * t + 1)
                dve.wait_ge(s["base_rdy"], g + 1)
                dve.wait_ge(s["rk_mm"], g + 1)
                if k == 3:
                    stt(base[:], ps_rk[:], STEP[k] / (SW * ST), base[:], ALU.mult, ALU.add).then_inc(s["next_raw"], 1)
                    dve.wait_ge(s["next_raw"], t + 1)
                    dve.tensor_scalar(q[0][:], base[:], -CLAMP, CLAMP, ALU.max, ALU.min).then_inc(s["q_rdy"], 1)
                else:
                    stt(q[k + 1][:], ps_rk[:], STEP[k] / (SW * ST), base[:], ALU.mult, ALU.add).then_inc(s["q_rdy"], 1)

            def sums(pos, i):
                k, st = i % STAGES, i // STAGES
                g, t = pos.tiles(GS, 0, i), pos.tiles(STEPS, 0, st)
                if k == 1:
                    dve.wait_ge(s["p_rdy"], pos.tiles(3 * STEPS, 0, 3 * st + 2))
                    stt(p[1][:], p[2][:], 2.0, p[1][:], ALU.mult, ALU.add).then_inc(s["psum1"], 1)
                if k == 2:
                    dve.wait_ge(s["third_rdy"], t + 1)
                    stt(q[1][:], q[1][:], 1.0 / 3.0, drv[st][:], ALU.mult, ALU.add).then_inc(s["qsum"], 1)
                if k == 3:
                    dve.wait_ge(s["psum3"], t + 1)
                    dve.wait_ge(s["w_rdy"], g + 1)
                    stt(p[1][:], p[1][:], 1.0 / 3.0, vel[:], ALU.mult, ALU.add).then_inc(s["psum4"], 1)
                    dve.wait_ge(s["psum4"], t + 1)
                    dve.tensor_scalar(p[0][:], p[1][:], -CLAMP * BETA - ALPHA, CLAMP * BETA - ALPHA, ALU.max,
                                      ALU.min).then_inc(s["p0_rdy"], 1)

            def tanh_rest(pos, i):
                dve.wait_ge(s["th_rdy"], pos.tiles(GS, 0, i + 2))
                stt(th[:, 1], tanh, ST, th[:, 0], ALU.mult, ALU.subtract).then_inc(s["tl_rdy"], 1)

            def state_rest(pos, st, off=0):
                cols = slice(st * B, (st + 1) * B)
                dve.wait_ge(s["qh_rdy"], pos.tiles(STEPS, off, st + 1))
                stt(qp[:, 1, :, cols], q[0][:], SX, qp[:, 0, :, cols], ALU.mult, ALU.subtract).then_inc(s["qp_rdy"], 1)

            def end_of_tile(pos):
                state_rest(pos, STEPS - 1, -1)
                if pos.tile > 1:
                    list_out(pos, -1)

            def routing(pos, numbers, skipped=0):
                lo, key, sc, z, zt, o1, o2 = (r[k][:] for k in "lo key sc z zt o1 o2".split())
                slot, nf, eq = lo, zt, key
                new = pre[0][:, 4:]
                for n in numbers:
                    if n > skipped:
                        dve.wait_ge(s["route"], pos.tiles(NROUTE, -1, n - skipped))
                    if n == 0:
                        dve.wait_ge(s["sc_rdy"], pos.tiles(1))
                        ins = dve.tensor_scalar(lo, z, -1.0, None, ALU.min)
                    if n == 1:
                        ins = dve.reciprocal(lo, lo)
                    if n == 2:
                        ins = tt(lo, zt, lo, ALU.mult)
                    if n == 3:
                        ins = stt(lo, z, -1.0, lo, ALU.is_lt, ALU.mult)
                    if n == 4:
                        ins = dve.tensor_scalar(sc, sc, 0.5, 0.5, ALU.mult, ALU.add)
                    if n == 5:
                        ins = stt(sc, z, -1.0, sc, ALU.is_ge, ALU.mult)
                    if n == 6:
                        ins = tt(sc, sc, lo, ALU.add)
                    if n == 7:
                        ins = tt(lo, sc, gb[:], ALU.add)
                    if n in (8, 13):
                        ins = dve.tensor_reduce(mx, lo, AXIS.X, ALU.max)
                    if n in (9, 14):
                        ins = stt(key, lo, mx, desc[:], ALU.is_equal, ALU.mult)
                    if n in (10, 15):
                        ins = dve.tensor_reduce(ix, key, AXIS.X, ALU.max)
                    if n in (11, 16):
                        ins = dve.tensor_scalar(o1 if n == 11 else o2, desc[:], ix, None, ALU.is_equal)
                    if n == 12:
                        ins = stt(lo, o1, -1e30, lo, ALU.mult, ALU.add)
                    if n == 17:
                        ins = tt(chosen[:], o1, o2, ALU.add)
                    if n == 18:
                        ins = tt(key, chosen[:], sc, ALU.mult)
                    if n == 19:
                        ins = dve.tensor_reduce(mx, key, AXIS.X, ALU.add)
                    if n == 20:
                        ins = dve.reciprocal(ix, mx)
                    if n == 21:
                        if pos.tile > 1:
                            dve.wait_ge(s["sent1"], pos.tiles(16, -1))
                            dve.wait_ge(s["sent2"], pos.tiles(16, -1))
                        dve.tensor_scalar(io[:, N + 1:], key, ix, 1.0 / (SW * SH), ALU.mult, ALU.mult)
                        dve.tensor_copy(io[:, N:N + 1].bitcast(I32), part).then_inc(s["tags_rdy"], 1)
                        ins = dve.tensor_scalar(part, part, float(P), None, ALU.add)
                    if n == 22:
                        dve.wait_ge(s["rank_mm"], pos.tiles(1))
                        ins = tt(slot, count[:], ps_l[:, RANK], ALU.add)
                    if n == 23:
                        ins = tt(zt, o1, slot, ALU.mult)
                    if n == 24:
                        dve.tensor_reduce(idx[:, 0:1], zt, AXIS.X, ALU.max)
                        ins = tt(key, o2, slot, ALU.mult)
                    if n == 25:
                        dve.tensor_reduce(idx[:, 1:2], key, AXIS.X, ALU.max).then_inc(s["idx_rdy"], 1)
                        ins = tt(count[:], count[:], ps_l[:, TOTAL], ALU.add)
                    if n == 26:
                        ins = tt(rem[:], rem[:], ps_l[:, TOTAL], ALU.add)
                    if n == 27:
                        ins = dve.tensor_scalar(new, rem[:], float(P), None, ALU.is_ge)
                    if n == 28:
                        ins = stt(rem[:], new, -float(P), rem[:], ALU.mult, ALU.add)
                    if n == ENTER:
                        ins = tt(pre[1][:, 4:], new, pre[0][:, 3:3 + E], ALU.add)
                    if n == 30:
                        ins = tt(pre[2][:, 4:], pre[1][:, 4:], pre[1][:, 2:2 + E], ALU.add)
                    if n == 31:
                        ins = tt(nf, pre[2][:, 4:], pre[2][:, 0:E], ALU.add)
                    if n == 32:
                        ins = stt(eq, nf, filled, new, ALU.add, ALU.subtract)
                    if n == 33:
                        ins = stt(eq, eq, slots_of, new, ALU.is_equal, ALU.mult)
                    if n == 34:
                        ins = tt(slot, eq, code[:], ALU.mult)
                    if n == 35:
                        ins = dve.tensor_reduce(lv[:, 0:1], slot, AXIS.X, ALU.add)
                    if n == 36:
                        ins = tt(slot, eq, eidx[:], ALU.mult)
                    if n == 37:
                        ins = dve.tensor_reduce(lv[:, 1:2], slot, AXIS.X, ALU.add)
                    if n == 38:
                        ins = tt(filled, filled, nf[:, E - 1:E], ALU.add)
                    if n == 39:
                        ins = stt(code[:], new, float(P), code[:], ALU.mult, ALU.add)
                    ins.then_inc(s["route"], 1)
                    if n == NROUTE - 1:
                        tt(lst, lst, lv, ALU.add).then_inc(s["list_rdy"], 1)

            def list_out(pos, off=0):
                dve.wait_ge(s["list_mm"], pos.tiles(1, off))
                dve.tensor_copy(todo[:], ps_l[0:1, LIST:LIST + 2 * SLOTS]).then_inc(s["todo_rdy"], 1)

            def hidden(pos, j):
                dve.wait_ge(s["sg_rdy"], pos.jobs(j) + 1)
                stt(hid[:], ps_u[:, 0:H], SH / (SW * SX), hid[:], ALU.mult, ALU.mult).then_inc(s["h_rdy"], 1)

            def hidden_rest(pos, j):
                dve.wait_ge(s["hth_rdy"], pos.jobs(j) + 1)
                tt(ht[:, 1], ps_t[:], ht[:, 0], ALU.subtract).then_inc(s["hts_rdy"], 1)

            def shared_out(pos):
                dve.wait_ge(s["y_mm"], pos.jobs(1) + 1)
                dve.wait_ge(s["res_in"], pos.tiles(16))
                stt(res[:], ps_y[:], 1.0 / (SW * SH), res[:], ALU.mult, ALU.add).then_inc(s["res_rdy"], 1)

            def tile_part(pos, chain, weights, ffn, experts, before=False, more=True):
                for i in range(GS):
                    k = i % STAGES
                    if chain:
                        base_of(pos, i, ffn)
                    elif ffn:
                        if i == 0:
                            end_of_tile(pos)
                        routing(pos, ROUTE_AT[i][0] + ROUTE_AT[i][1])
                    if chain and i == STAGES:
                        state_rest(pos, 0)
                    if ffn and i == 3 or experts and i == 7:
                        hidden(pos, i // 2)
                    if ffn:
                        routing(pos, ROUTE_AT[i][2])
                    if weights:
                        for n in PIECES_AT[i][:-1]:
                            piece_lo(dve, pos, n)
                    if chain:
                        next_state(pos, i)
                        sums(pos, i)
                        if k == 0 and (i == 0 or more):
                            drive_of(pos if i == 0 else Pos(**{**vars_of(pos), "tile": pos.tile + 1}), 1 if i == 0 else 0)
                    if ffn and i == 1 or experts and i == 5:
                        hidden(pos, i // 2)
                    if before and i == 0:
                        hidden_rest(pos, -1)
                    if ffn and i in (2, 4):
                        hidden_rest(pos, i // 2 - 1)
                    if experts and i == 6:
                        hidden_rest(pos, 2)
                    if weights:
                        for n in PIECES_AT[i][-1:]:
                            piece_lo(dve, pos, n)
                    if chain:
                        tanh_rest(pos, i)
                    if ffn and i == 5:
                        shared_out(pos)

            def tail_part(pos, flush=False):
                for x in range(2):
                    if flush and x == 1:
                        list_out(ENDING, 1)
                    hidden(pos, x)
                    hidden_rest(pos, x)

            dve.wait_ge(s["set_up"], 1)
            drive_of(START, 0)
            tile_part(START, True, True, False, False)
            dve.wait_ge(s["stored"], 16)
            tile_part(FIRSTS, True, True, True, False)
            with dve.Fori(0, WTILES - 2) as it:
                tile_part(Pos(it=it, **TAKING), True, True, True, False)
            tile_part(BEFORE, True, False, True, False)
            tile_part(FIRSTX, True, False, True, True)
            with dve.Fori(0, NMAIN - 1) as it:
                tile_part(Pos(it=it, **MAIN), True, False, True, True, True)
            tile_part(MAINEND, True, False, True, True, True, False)
            tile_part(ENDING, False, False, True, True, True)
            list_out(ENDING)
            pos = Pos(**TAIL)
            hidden_rest(pos, -1)
            dve.wait_ge(s["todo_rdy"], TILES)
            dve.tensor_scalar(fill_idx[:], count[:], slots_of, None, ALU.add).then_inc(s["fill_rdy"], 1)
            dve.tensor_scalar(pre[0][:, 4:], rem[:], 0.5, None, ALU.is_ge).then_inc(s["route"], 1)
            routing(Pos(TILES + 1), range(ENTER, NROUTE), ENTER - 1)
            tail_part(pos, True)
            with dve.Fori(0, NTAIL - 1) as it:
                tail_part(Pos(it=it, **REST))

        @block.tensor
        def _(pe):
            mm = pe.matmul

            def chain_of(pos, i):
                pe.wait_ge(s["tl_rdy"], pos.tiles(GS, 0, i + 1))
                for o in range(NC):
                    for k in range(NC):
                        hi, lo = (cw[:, a, k, o * P:(o + 1) * P] for a in range(2))
                        mm(ps_rk[:, o], hi, th[:, 0, k], start=k == 0, stop=False)
                        mm(ps_rk[:, o], hi, th[:, 1, k], start=False, stop=False)
                        last = mm(ps_rk[:, o], lo, th[:, 0, k], start=False, stop=k == NC - 1)
                last.then_inc(s["rk_mm"], 1)

            PAIRS = ((0, 0), (0, 1), (1, 0))

            def router(pos):
                pe.wait_ge(s["qp_rdy"], pos.tiles(STEPS))
                for k in range(NC):
                    for a, b in PAIRS:
                        last = mm(ps_l[:, LOGIT], qp[:, a, k], gw[:, b, k], start=k == 0 and a == b,
                                  stop=k == NC - 1 and a == 1)
                last.then_inc(s["lg_mm"], 1)

            def up_of(pos, j, x, weights):
                for k in range(NC):
                    for a, b in PAIRS:
                        for half, ps in enumerate((ps_g, ps_u)):
                            last = mm(ps[:, 0:H], x[:, a, k], weights(P, b, (2 * k + half) * H, H),
                                      start=k == 0 and a == b, stop=k == NC - 1 and a == 1)
                last.then_inc(s["up_mm"], 1)

            def turn_of(pos, j):
                pe.wait_ge(s["h_rdy"], pos.jobs(j) + 1)
                for k, (h0, hn) in enumerate(HK):
                    last = pe.transpose(ps_t[0:hn, k], hid[:, h0:h0 + hn], ident[:])
                last.then_inc(s["ht_mm"], 1)

            def down_of(pos, j, weights, first=True, final=True):
                pe.wait_ge(s["hts_rdy"], pos.jobs(j) + 1)
                for k, (_, hn) in enumerate(HK):
                    for a, b in PAIRS:
                        last = mm(ps_y[:], ht[0:hn, a, k], weights(hn, b, UP + k * N, N),
                                  start=first and k == 0 and a == b, stop=final and k == len(HK) - 1 and a == 1)
                last.then_inc(s["y_mm"], 1)

            def shared(a):
                return lambda pp, b, c, n: w[0:pp, E + a, b, c:c + n]

            def expert(e):
                return lambda pp, b, c, n: w[0:pp, bass.ds(e, 1), b, c:c + n].rearrange("p o c -> p (o c)")

            def rows_turn(pos):
                for a in range(2):
                    for k in range(NC):
                        last = pe.transpose(ps_x[:, a * NC + k], qp[:, a, k], ident16[:])
                last.then_inc(s["rows_mm"], 1)

            def expert_turn(pos, x):
                pe.wait_ge(s["x_in_rdy"], pos.xjobs(x, 16, 16))
                for c in range(2 * NC):
                    last = pe.transpose(ps_x[:, c], x_in[:, 0:N].bitcast(F16)[:, c * P:(c + 1) * P], ident16[:])
                last.then_inc(s["xt_mm"], 1)

            def ranks(pos):
                pe.wait_ge(s["tags_rdy"], pos.tiles(1))
                mm(ps_l[:, RANK], upper[:], chosen[:], start=True, stop=True)
                mm(ps_l[:, TOTAL], ones[:], chosen[:], start=True, stop=True).then_inc(s["rank_mm"], 1)

            def list_row(pos, off=0):
                pe.wait_ge(s["list_rdy"], pos.tiles(1, off))
                for c in range(2):
                    last = mm(ps_l[0:1, LIST + c * SLOTS:LIST + (c + 1) * SLOTS], lst[:, c:c + 1], ident[:, 0:SLOTS],
                              start=True, stop=True)
                last.then_inc(s["list_mm"], 1)

            def experts_of(pos, x0):
                at, n = pos.xjobs(x0, 1, SLOTS), 2 - x0
                _, found = nc.values_load_multi_w_load_instructions(
                    todo[0:1, bass.ds(at, n)] if pos.it is not None else todo[0:1, at:at + n],
                    engines=[mybir.EngineType.PE], min_val=0, max_val=E - 1)
                return dict(zip(range(x0, 2), found))

            def tile_part(pos, chain, ffn, experts, before):
                for i in range(GS):
                    if chain:
                        chain_of(pos, i)
                    if ffn and i == 0:
                        if pos.tile > 1:
                            pe.wait_ge(s["todo_rdy"], pos.tiles(1, -1))
                        router(pos)
                        if experts:
                            e = experts_of(pos, -1 if before else 0)
                        up_of(pos, 0, qp, shared(0))
                    if ffn and i == 1:
                        rows_turn(pos)
                        if before:
                            pe.wait_ge(s["y_rdy"], pos.xjobs(-1))
                            down_of(pos, -1, expert(e[-1]))
                        turn_of(pos, 0)
                    if ffn and i == 2:
                        up_of(pos, 1, qp, shared(1))
                    if ffn and i == 3:
                        if experts:
                            pe.wait_ge(s["rows_rdy"], pos.tiles(1))
                            expert_turn(pos, 0)
                        if before:
                            pe.wait_ge(s["y_rdy"], pos.xjobs(0))
                        down_of(pos, 0, shared(0), final=False)
                        turn_of(pos, 1)
                    if experts and i == 4:
                        pe.wait_ge(s["x_t_rdy"], pos.xjobs(0, 1, 1))
                        up_of(pos, 2, x_t, expert(e[0]))
                    if ffn and i == 4:
                        ranks(pos)
                    if experts and i == 5:
                        expert_turn(pos, 1)
                    if ffn and i == 5:
                        down_of(pos, 1, shared(1), first=False)
                    if experts and i == 5:
                        turn_of(pos, 2)
                    if experts and i == 6:
                        pe.wait_ge(s["x_t_rdy"], pos.xjobs(1, 1, 1))
                        up_of(pos, 3, x_t, expert(e[1]))
                    if experts and i == 7:
                        pe.wait_ge(s["res_rdy"], pos.tiles(1))
                        down_of(pos, 2, expert(e[0]))
                        turn_of(pos, 3)
                    if ffn and i == 7:
                        list_row(pos)

            def tail_part(pos, e, final=False):
                for x in range(2):
                    pe.wait_ge(s["x_t_rdy"], pos.xjobs(x, 1, 1))
                    up_of(pos, x, x_t, expert(e[x]))
                    if not (final and x == 1):
                        expert_turn(pos, x + 1)
                    pe.wait_ge(s["y_rdy"], pos.xjobs(x - 1))
                    down_of(pos, x - 1, expert(e[x - 1]))
                    turn_of(pos, x)

            pe.wait_ge(s["set_up"], 1)
            pe.wait_ge(s["w_lo"], FIRST)
            tile_part(START, True, False, False, False)
            pe.wait_ge(s["w_lo"], FIRST + PT)
            tile_part(FIRSTS, True, True, False, False)
            with pe.Fori(0, WTILES - 2) as it:
                tile_part(Pos(it=it, **TAKING), True, True, False, False)
            tile_part(BEFORE, True, True, False, False)
            pe.wait_ge(s["w_lo"], FIRST + WTILES * PT)
            tile_part(FIRSTX, True, True, True, False)
            with pe.Fori(0, NMAIN) as it:
                tile_part(Pos(it=it, **MAIN), True, True, True, True)
            tile_part(ENDING, False, True, True, True)
            pe.wait_ge(s["todo_rdy"], TILES)
            pos = Pos(**TAIL)
            e = experts_of(pos, -1)
            expert_turn(pos, 0)
            pe.wait_ge(s["x_t_rdy"], pos.xjobs(0, 1, 1))
            up_of(pos, 0, x_t, expert(e[0]))
            expert_turn(pos, 1)
            pe.wait_ge(s["y_rdy"], pos.xjobs(-1))
            down_of(pos, -1, expert(e[-1]))
            turn_of(pos, 0)
            list_row(ENDING, 1)
            pe.wait_ge(s["x_t_rdy"], pos.xjobs(1, 1, 1))
            up_of(pos, 1, x_t, expert(e[1]))
            pe.wait_ge(s["y_rdy"], pos.xjobs(0))
            down_of(pos, 0, expert(e[0]))
            turn_of(pos, 1)
            pe.wait_ge(s["todo_rdy"], TILES + 1)
            expert_turn(pos, 2)
            with pe.Fori(0, NTAIL - 2) as it:
                pos = Pos(it=it, **REST)
                tail_part(pos, experts_of(pos, -1))
            tail_part(LASTS, experts_of(LASTS, -1), True)
            end = Pos(0, jobs=TAIL["jobs"] + 2 * NTAIL, xjobs=SLOTS)
            pe.wait_ge(s["y_rdy"], SLOTS - 1)
            down_of(end, -1, expert(experts_of(LASTS, -1)[1]))


def kernel(x, cond_2048, L0_cond_coupling, L0_cond_bias, L0_ffn_gate_w, L0_ffn_gate_bias, L0_ffn_shared_gw,
           L0_ffn_shared_dw, L0_ffn_up_w, L0_ffn_down_w):
    import concourse.bacc as _bacc
    from concourse.bass_utils import run_bass_kernel_spmd as _run

    def split(a, n):
        return np.ascontiguousarray(a.reshape(n, P, -1).transpose(1, 0, 2))

    x, cond_2048 = np.asarray(x), np.asarray(cond_2048)
    xt = x.transpose(1, 0, 2)
    sg, sd = np.asarray(L0_ffn_shared_gw), np.asarray(L0_ffn_shared_dw)
    ups = [np.asarray(u) for u in np.asarray(L0_ffn_up_w)]
    downs = [np.asarray(d) for d in np.asarray(L0_ffn_down_w)]
    for i in range(2):
        half = slice(i * H, (i + 1) * H)
        ups.append(np.concatenate([sg[2 * H:][half], sg[:2 * H][half]]))
        downs.append(sd[:, half])
    arrays = {
        "in_drive": np.ascontiguousarray(xt.reshape(T, B, NC, P).transpose(0, 3, 2, 1)),
        "in_cond": np.ascontiguousarray(cond_2048.reshape(B, NC, P).transpose(2, 1, 0)),
        "in_rows": np.ascontiguousarray(xt.reshape(T * B, N)),
        "in_coupling": split(np.asarray(L0_cond_coupling).T, NC),
        "in_bias": np.ascontiguousarray(np.asarray(L0_cond_bias).reshape(NC, P).T),
        "in_gate": split(np.asarray(L0_ffn_gate_w).T, NC).reshape(P, NC * E),
        "in_gate_bias": np.ascontiguousarray(np.asarray(L0_ffn_gate_bias)),
        "in_up": np.stack([split(u.T, NC).reshape(P, UP) for u in ups]),
        "in_down": np.stack([np.ascontiguousarray(d.T) for d in downs]),
    }
    nc = _bacc.Bacc("TRN2", target_bir_lowering=False, num_devices=1)
    aps = [nc.dram_tensor(n, a.shape, F32, kind="ExternalInput").ap() for n, a in arrays.items()]
    out = nc.dram_tensor("result", (TOKENS + P, N), F32, kind="ExternalOutput").ap()
    xs = nc.dram_tensor("expert_rows", (NO_ROWS + P, ROW), F32, kind="Internal").ap()
    build(nc, *aps, out, xs)
    r = _run(nc, [arrays], core_ids=[0])
    return np.ascontiguousarray(r.results[0]["result"][:TOKENS].reshape(T, B, N).transpose(1, 0, 2))
```

```python
from contextlib import ExitStack

import numpy as np

import concourse.bass as bass
from concourse import mybir

F32 = mybir.dt.float32
F16 = mybir.dt.float16
I32 = mybir.dt.int32
ACT = mybir.ActivationFunctionType
ALU = mybir.AluOpType
AXIS = mybir.AxisListType

P = 128
B, T, N = 64, 64, 512
NC = N // P
E = 8
H = 352
TOKENS = B * T
TILES = TOKENS // P
STEPS = P // B
STAGES = 4
GS = STEPS * STAGES
UP = NC * 2 * H
HK = [(k, min(P, H - k)) for k in range(0, H, P)]
WC = UP + len(HK) * N

DT, EPS, ALPHA, BETA, CLAMP = 0.01, 0.08, 0.7, 0.8, 20.0
STEP = [DT / 2, DT / 2, DT, DT / 6]

SW = 2.0 ** 8
SX = 2.0 ** 11
ST = 2.0 ** 15
SH = 2.0 ** 4

ROW = N + 1 + E
REGION = TOKENS + P
NO_ROWS = E * REGION
SLOTS = (TOKENS * 2 + E * (P - 1)) // P + 1
LAG = 5
XFIRST = 2 * (TILES - LAG)


def full_tiles(tiles):
    return -(-(2 * P * tiles - E * (P - 1)) // P)


assert full_tiles(LAG) >= 2 and full_tiles(TILES - 1) >= XFIRST + 1 and full_tiles(TILES) >= XFIRST + 2

PIECES = [(c, min(N, UP - c), P) for c in range(0, UP, N)] + [(UP + k * N, N, HK[k][1]) for k in range(len(HK))]
PT = 2 * len(PIECES)
FIRST = NC + 1
WTILES = (E + 2) // 2
STG = 3
PIECES_OF = (3,2,2,2,2,3,2,2)
PIECES_AT = [range(sum(PIECES_OF[:i]), sum(PIECES_OF[:i + 1])) for i in range(GS)]
BY_POOL = [n in [at[-1] for at in PIECES_AT] for n in range(PT)]
assert PT % STG == 0
SPLIT_LATE = (0, 5, 6)
ROUTE_AT = [((), (), (), (), ()),
            ((), (0,), (1, 2, 3), (4,), (5,)),
            ((6,), (7,), (8, 9), (10,), (11,)),
            ((12,), (13,), (14,), (15,), (16,)),
            ((17,), (18,), (19, 20, 21), (), ()),
            ((), (), (22, 23, 24), (25,), (26,)),
            ((27,), (28,), (29, 30, 31, 32), (33,), (34,)),
            ((35,), (36,), (37, 38, 39), (), ())]
NROUTE, ENTER = 40, 29


class Pos:

    def __init__(self, tile, jobs=0, xjobs=0, jpt=0, xpt=0, it=None):
        self.tile, self.jobs0, self.x0, self.jpt, self.xpt, self.it = tile, jobs, xjobs, jpt, xpt, it

    def _at(self, per, base):
        return base if self.it is None or per == 0 else self.it * per + base

    def tiles(self, per, off=0, local=0):
        return self._at(per, per * (self.tile + off) + local)

    def jobs(self, j):
        return self._at(self.jpt, self.jobs0 + j)

    def pairs(self, x, per, local=0):
        return self._at(per * self.xpt // 2, per * ((self.x0 + x) // 2) + local)

    def xjobs(self, x, per=1, local=0):
        return self._at(self.xpt * per, per * (self.x0 + x) + local)


START = Pos(0)
FIRSTS = Pos(1)
TAKING = dict(tile=2, jobs=2, jpt=2)
BEFORE = Pos(WTILES, jobs=2 * (WTILES - 1))
FIRSTX = Pos(LAG + 1, jobs=2 * LAG)
MAIN = dict(tile=LAG + 2, jobs=2 * LAG + 4, xjobs=2, jpt=4, xpt=2)
NMAIN = TILES - LAG - 2
MAINEND = Pos(TILES - 1, jobs=2 * LAG + 4 * NMAIN, xjobs=2 * NMAIN)
ENDING = Pos(TILES, jobs=2 * LAG + 4 * (TILES - LAG - 1), xjobs=XFIRST - 2)
TAIL = dict(tile=TILES + 1, jobs=2 * LAG + 4 * (TILES - LAG), xjobs=XFIRST, jpt=2, xpt=2)
REST = dict(TAIL, jobs=TAIL["jobs"] + 2, xjobs=TAIL["xjobs"] + 2)
NTAIL = (SLOTS - XFIRST) // 2
LASTS = Pos(TILES + 1, jobs=TAIL["jobs"] + 2 * (NTAIL - 1), xjobs=SLOTS - 2)
assert WTILES == LAG and SLOTS % 2 == 0


def build(nc, drive, cond, rows, coupling, bias, gate, gate_bias, up, down, out, xs):
    with ExitStack() as ctx:
        def sb(name, shape, dt=F32):
            return ctx.enter_context(nc.sbuf_tensor(name, shape, dt))

        def pb(name, shape, dt=F32):
            return ctx.enter_context(nc.psum_tensor(name, shape, dt))

        w = sb("w", [P, E + 2, 2, WC], F16)
        cw = sb("cw", [P, 2, NC, N], F16)
        gw = sb("gw", [P, 2, NC, E], F16)
        gb = sb("gb", [P, E])
        bias_sb = sb("bias_sb", [P, NC])
        q = [sb(f"q{i}", [P, NC, B]) for i in range(3)]
        p = [sb(f"p{i}", [P, NC, B]) for i in range(3)]
        q, p = q + [q[2]], p + [p[2]]
        base = sb("base", [P, NC, B])
        vel = sb("vel", [P, NC, B])
        ref = sb("ref", [P, NC, B])
        th = sb("th", [P, 2, NC, B], F16)
        drv = [sb(f"drv{i}", [P, NC, B]) for i in range(STEPS)]
        qp = sb("qp", [P, 2, NC, P], F16)
        hid = sb("hid", [P, H])
        ht = sb("ht", [P, 2, len(HK), P], F16)
        io = sb("io", [P, ROW])
        x_in = sb("x_in", [P, N])
        res = sb("res", [P, N])
        x_t = sb("x_t", [P, 2, NC, P], F16)
        y = sb("y", [P, N])
        ident = sb("ident", [P, P])
        ident16 = sb("ident16", [P, P], F16)
        upper = sb("upper", [P, P], F16)
        ones = sb("ones", [P, P], F16)
        desc = sb("desc", [P, E])
        r = {k: sb("r_" + k, [P, E]) for k in "sc z zt lo key o1 o2".split()}
        chosen = sb("chosen", [P, E], F16)
        pre = [sb(f"pre{i}", [P, E + 4]) for i in range(3)]
        count = sb("count", [P, E])
        rem = sb("rem", [P, E])
        code = sb("code", [P, E])
        eidx = sb("eidx", [P, E])
        cols = sb("cols", [P, 11])
        mx, ix, part, slots_of, filled = (cols[:, c:c + 1] for c in range(5))
        lst, lv = cols[:, 5:7], cols[:, 7:9]
        idx = sb("idx", [P, 2], I32)
        fill_idx = r["o1"][:].bitcast(I32)
        todo = sb("todo", [1, 2 * SLOTS], I32)
        tok = [sb(f"tok{i}", [P, 1], I32) for i in range(2)]
        ws = [cols[:, 9 + i:10 + i] for i in range(2)]

        ps_rk = pb("ps_rk", [P, NC, B])
        ps_g = pb("ps_g", [P, 512])
        ps_u = pb("ps_u", [P, 512])
        ps_t = pb("ps_t", [P, len(HK), P])
        ps_y = pb("ps_y", [P, N])
        ps_l = pb("ps_l", [P, 512])
        ps_x = pb("ps_x", [P, 2 * NC, P], F16)
        tanh = pb("tanh", [P, 2, NC, B])[:, 0]
        LOGIT, RANK, TOTAL, LIST = slice(0, E), slice(16, 16 + E), slice(32, 32 + E), 64

        names = ("blank cond_in consts_in consts set_up zeroed bias_rdy "
                 "w_in0 w_in1 w_in2 w_in3 w_in4 w_hi w_lo w_scaled w_lo_pool "
                 "tanh_rdy th_rdy tl_rdy sq_rdy rk_mm cubic_rdy base_rdy next_raw q_rdy "
                 "v_rdy w_rdy p_rdy p0_rdy half_base ref_rdy ref2_rdy z_rdy third_rdy drv_in0 drv_in1 d_rdy "
                 "qsum psum1 psum3 psum3a psum4 qh_rdy qp_rdy "
                 "up_mm sg_rdy h_rdy ht_mm hth_rdy hts_rdy y_mm lg_mm sc_rdy route "
                 "chosen_rdy rank_mm idx_rdy list_rdy list_mm todo_rdy "
                 "rows_mm rows_rdy tags_rdy sending sent1 sent2 stored res_in res_rdy "
                 "x_in_rdy xt_mm x_t_rdy tag_in0 tag_in1 y_rdy y_free fill_rdy fill_in filled_up").split()
        s = {n: ctx.enter_context(nc.semaphore(n)) for n in names}
        stage_buf = [x_in[:], y[:], x_t[:].rearrange("p a b c -> p (a b c)").bitcast(F32)]

        def p_ready(eng, pos, i):
            k, st = i % STAGES, i // STAGES
            if k == 0:
                eng.wait_ge(s["p0_rdy"], pos.tiles(STEPS, 0, st + 1))
            else:
                eng.wait_ge(s["p_rdy"], pos.tiles(3 * STEPS, 0, 3 * st + k))

        def piece(pos, n):
            which, (c, cols, pp) = n // len(PIECES), PIECES[n % len(PIECES)]
            if pos.it is None:
                e = which + (2 * (pos.tile - 1) if pos.tile else E)
                h0 = HK[(c - UP) // N][0] if c >= UP else 0
                src = up[e, :, c:c + cols] if c < UP else down[e, h0:h0 + pp, :]
                return src, pp, cols, w[0:pp, e, 0, c:c + cols], w[0:pp, e, 1, c:c + cols]
            e = pos.it * 2 + (2 * (pos.tile - 1) + which)
            if c < UP:
                src = up[bass.ds(e, 1), :, c:c + cols].rearrange("o p c -> (o p) c")
            else:
                h0 = HK[(c - UP) // N][0]
                src = down[bass.ds(e, 1), h0:h0 + pp, :].rearrange("o p c -> (o p) c")
            hi, lo = (w[0:pp, bass.ds(e, 1), a, c:c + cols].rearrange("p o c -> p (o c)") for a in range(2))
            return src, pp, cols, hi, lo

        def split_wait(eng, pos, n):
            if n < 0 and pos.it is None and pos.tile == 0:
                eng.wait_ge(s["w_lo"], STG + n + 1)
                return
            off, n = (0, n) if n >= 0 else (-1, n + PT)
            upto = sum(BY_POOL[m] == BY_POOL[n] for m in range(n + 1))
            if BY_POOL[n]:
                eng.wait_ge(s["w_lo_pool"], pos.tiles(sum(BY_POOL), off, upto))
            else:
                eng.wait_ge(s["w_lo"], pos.tiles(PT - sum(BY_POOL), off, FIRST + upto))

        def all_split(eng, tiles):
            eng.wait_ge(s["w_lo"], FIRST + tiles * (PT - sum(BY_POOL)) if tiles else NC)
            if tiles:
                eng.wait_ge(s["w_lo_pool"], tiles * sum(BY_POOL))

        def piece_load(eng, pos, n):
            src, pp, cols, _, _ = piece(pos, n)
            b = n % STG
            split_wait(eng, pos, n - STG)
            eng.dma_start(stage_buf[b][0:pp, 0:cols], src).then_inc(s[f"w_in{b}"], 16)

        def piece_hi(eng, pos, n):
            _, pp, cols, hi, _ = piece(pos, n)
            b = n % STG
            eng.wait_ge(s[f"w_in{b}"], pos.tiles(PT // STG * 16, 0, 16 * (n // STG + 2)))
            eng.activation(hi, stage_buf[b][0:pp, 0:cols], ACT.Copy, scale=SW).then_inc(s["w_hi"], 1)
            if BY_POOL[n]:
                eng.activation(stage_buf[b][0:pp, 0:cols], stage_buf[b][0:pp, 0:cols], ACT.Copy,
                               scale=SW).then_inc(s["w_scaled"], 1)

        def piece_lo(eng, pos, n):
            _, pp, cols, hi, lo = piece(pos, n)
            b = n % STG
            if BY_POOL[n]:
                eng.wait_ge(s["w_scaled"], pos.tiles(sum(BY_POOL), 0, sum(BY_POOL[:n + 1])))
                eng.tensor_tensor(lo, stage_buf[b][0:pp, 0:cols], hi, ALU.subtract).then_inc(s["w_lo_pool"], 1)
                return
            eng.wait_ge(s["w_hi"], pos.tiles(PT, 0, FIRST + n + 1))
            eng.scalar_tensor_tensor(lo, stage_buf[b][0:pp, 0:cols], SW, hi, ALU.mult,
                                     ALU.subtract).then_inc(s["w_lo"], 1)

        first_buf = stage_buf + [qp[:].rearrange("p a b c -> p (a b c)").bitcast(F32), hid[:]]
        first_pieces = [(coupling[:, k, :], N, cw[:, 0, k, :], cw[:, 1, k, :]) for k in range(NC)]
        first_pieces.append((gate, NC * E, gw[:, 0].rearrange("p a b -> p (a b)"), gw[:, 1].rearrange("p a b -> p (a b)")))

        block = ctx.enter_context(nc.Block())

        @block.sync
        def _(sp):
            sp.dma_start(q[0][:], cond).then_inc(s["cond_in"], 16)
            for n, (src, cols, _, _) in enumerate(first_pieces):
                sp.dma_start(first_buf[n][:, 0:cols], src).then_inc(s[f"w_in{n}"], 16)
            sp.dma_start(bias_sb[:], bias).then_inc(s["consts_in"], 16)
            sp.dma_start(gb[:], gate_bias.rearrange("(a n) -> a n", a=1).to_broadcast([P, E])).then_inc(s["consts_in"], 16)
            for t in range(STEPS):
                sp.dma_start(drv[t][:], drive[t]).then_inc(s[f"drv_in{t}"], 16)
            sp.wait_ge(s["zeroed"], 1)
            sp.dma_start(out[TOKENS:TOKENS + P, :], res[:]).then_inc(s["blank"], 16)
            sp.wait_ge(s["set_up"], 1)
            sp.dma_start(xs[NO_ROWS:NO_ROWS + P, :], io[:]).then_inc(s["stored"], 16)

            def drive_in(pos, st):
                t = pos.tiles(STEPS, 0, st + STEPS)
                src = drive[t] if pos.it is None else drive[bass.ds(t, 1)].rearrange("o p c b -> (o p) c b")
                sp.wait_ge(s["qsum"], pos.tiles(3 * STEPS, 0, 3 * st + 2))
                sp.dma_start(drv[st][:], src).then_inc(s[f"drv_in{st}"], 16)

            def expert_rows_in(pos, x, row):
                if pos.it is not None or pos.x0 + x > 0:
                    sp.wait_ge(s["xt_mm"], pos.xjobs(x, 1, 0))
                sp.dma_start(x_in[:], xs[bass.ds(row, P), 0:N]).then_inc(s["x_in_rdy"], 16)

            def expert_tags_in(pos, x, row, e):
                if pos.it is not None or pos.x0 + x >= 2:
                    sp.wait_ge(s["y_free"], pos.xjobs(x, 16, -16))
                tag_in = s[f"tag_in{x % 2}"]
                sp.dma_start(tok[x % 2][:].bitcast(F32), xs[bass.ds(row, P), N:N + 1],
                             allow_slow_non_contiguous=True).then_inc(tag_in, 16)
                sp.dma_start(ws[x % 2], xs[bass.ds(row, P), bass.ds(e + (N + 1), 1)],
                             allow_slow_non_contiguous=True).then_inc(tag_in, 16)

            def listed(pos, x0, x1, off, most):
                at, n = pos.xjobs(x0, 1, off), x1 - x0
                _, found = nc.values_load_multi_w_load_instructions(
                    todo[0:1, bass.ds(at, n)] if pos.it is not None else todo[0:1, at:at + n],
                    engines=[mybir.EngineType.SP], min_val=0, max_val=most)
                return dict(zip(range(x0, x1), found))

            def rows_of(pos, x0, x1):
                return listed(pos, x0, x1, 0, NO_ROWS)

            def experts_of(pos, x0, x1):
                return listed(pos, x0, x1, SLOTS, E - 1)

            def residual_in(pos):
                r0 = pos.tiles(P, -1)
                src = rows[bass.ds(r0, P), :] if pos.it is not None else rows[r0:r0 + P, :]
                sp.wait_ge(s["stored"], pos.tiles(16))
                sp.dma_start(res[:], src).then_inc(s["res_in"], 16)

            def result_out(pos):
                r0 = pos.tiles(P, -1)
                dst = out[bass.ds(r0, P), :] if pos.it is not None else out[r0:r0 + P, :]
                sp.wait_ge(s["res_rdy"], pos.tiles(1))
                sp.dma_start(dst, res[:]).then_inc(s["stored"], 16)

            def tile_part(pos, chain, weights, ffn, experts, last=False):
                if experts:
                    sp.wait_ge(s["todo_rdy"], pos.tiles(1, -1))
                    row = rows_of(pos, 0, 3 if last else 2)
                    sp.wait_ge(s["sent1"], pos.tiles(16, -1))
                    sp.wait_ge(s["sent2"], pos.tiles(16, -1))
                    expert_rows_in(pos, 0, row[0])
                    e = experts_of(pos, 0, 3 if last else 2)
                for i in range(GS):
                    if weights:
                        for n in PIECES_AT[i]:
                            piece_load(sp, pos, n)
                    if ffn and i == 1:
                        residual_in(pos)
                    if chain and i == 3:
                        drive_in(pos, 0)
                    if experts and i == 3:
                        expert_rows_in(pos, 1, row[1])
                        expert_tags_in(pos, 0, row[0], e[0])
                    if ffn and i == 6:
                        result_out(pos)
                    if chain and i == 7:
                        drive_in(pos, 1)
                    if experts and i == 7:
                        expert_tags_in(pos, 1, row[1], e[1])
                    if last and i == 6:
                        sp.wait_ge(s["sent1"], 16 * TILES)
                        sp.wait_ge(s["sent2"], 16 * TILES)
                        sp.dma_start(io[:], xs[NO_ROWS:NO_ROWS + P, :]).then_inc(s["fill_in"], 16)
                    if last and i == 7:
                        expert_rows_in(pos, 2, row[2])
                return (row[2], e[2]) if last else None

            tile_part(START, True, True, False, False)
            sp.wait_ge(s["blank"], 16)
            tile_part(FIRSTS, True, True, True, False)
            with sp.Fori(0, WTILES - 2) as it:
                tile_part(Pos(it=it, **TAKING), True, True, True, False)
            tile_part(BEFORE, True, False, True, False)
            all_split(sp, WTILES)
            tile_part(FIRSTX, True, False, True, True)
            with sp.Fori(0, NMAIN - 1) as it:
                tile_part(Pos(it=it, **MAIN), True, False, True, True)
            last = dict(MAIN, tile=MAIN["tile"] + NMAIN - 1, jobs=MAIN["jobs"] + 4 * (NMAIN - 1),
                        xjobs=MAIN["xjobs"] + 2 * (NMAIN - 1))
            tile_part(Pos(**last), False, False, True, True)
            third_job = tile_part(ENDING, False, False, True, True, True)
            sp.wait_ge(s["todo_rdy"], TILES)
            pos = Pos(**TAIL)
            expert_rows_in(pos, 1, rows_of(pos, 1, 2)[1])
            expert_tags_in(pos, 0, *third_job)
            sp.wait_ge(s["filled_up"], 16 * E)
            sp.wait_ge(s["todo_rdy"], TILES + 1)
            with sp.Fori(0, NTAIL - 1) as it:
                pos = Pos(it=it, **REST)
                row = rows_of(pos, -1, 2)
                expert_rows_in(pos, 0, row[0])
                e = experts_of(pos, -1, 1)
                expert_tags_in(pos, -1, row[-1], e[-1])
                expert_rows_in(pos, 1, row[1])
                expert_tags_in(pos, 0, row[0], e[0])
            end = Pos(0, xjobs=SLOTS)
            expert_tags_in(end, -1, rows_of(end, -1, 0)[-1], experts_of(end, -1, 0)[-1])
            sp.wait_ge(s["y_free"], 16 * SLOTS)

        @block.gpsimd
        def _(pool):
            tt = pool.tensor_tensor
            pool.memset(res[:], 0.0).then_inc(s["zeroed"], 1)
            pool.memset(ident[:], 0.0)
            pool.memset(ident16[:], 0.0)
            pool.memset(ones[:], 1.0)
            pool.memset(upper[:], 1.0).then_inc(s["consts"], 1)
            pool.wait_ge(s["consts"], 1)
            for mat in (ident, ident16):
                pool.affine_select(out=mat[:], in_=mat[:], compare_op=ALU.not_equal, fill=1.0, base=0,
                                   pattern=[[-1, P]], channel_multiplier=1)
            pool.affine_select(out=upper[:], in_=upper[:], compare_op=ALU.is_gt, fill=0.0, base=0,
                               pattern=[[1, P]], channel_multiplier=-1)
            pool.iota(idx[:, 0:1], pattern=[[0, 1]], base=0, channel_multiplier=1)
            pool.memset(io[:], 0.0)
            for e in range(E):
                pool.memset(desc[:, e:e + 1], float(E - e))
                pool.memset(eidx[:, e:e + 1], float(e))
                pool.memset(count[:, e:e + 1], float(e * REGION))
                pool.memset(code[:, e:e + 1], float(e * REGION - NO_ROWS))
            for t in (rem[:], filled, lst[:, 1:2], *(t[:] for t in pre)):
                pool.memset(t, 0.0)
            pool.memset(lst[:, 0:1], float(NO_ROWS)).then_inc(s["consts"], 1)
            pool.wait_ge(s["consts"], 2)
            pool.tensor_copy(slots_of, idx[:, 0:1])
            pool.tensor_copy(part, idx[:, 0:1]).then_inc(s["consts"], 1)
            pool.wait_ge(s["consts"], 3)
            pool.tensor_scalar(io[:, N:N + 1].bitcast(I32), part, float(TOKENS), None, ALU.add).then_inc(s["set_up"], 1)

            def stage(pos, i):
                k, st = i % STAGES, i // STAGES
                g, t = pos.tiles(GS, 0, i), pos.tiles(STEPS, 0, st)
                pool.wait_ge(s["q_rdy"], g + 1)
                if k == 0:
                    pool.wait_ge(s["d_rdy"], t + 1)
                    tt(ref[:], q[0][:], drv[st][:], ALU.add).then_inc(s["ref_rdy"], 1)
                p_ready(pool, pos, i)
                tt(vel[:], q[k][:], p[k][:], ALU.subtract).then_inc(s["v_rdy"], 1)
                if k == 2:
                    pool.wait_ge(s["psum1"], t + 1)
                    pool.wait_ge(s["base_rdy"], g + 1)
                if k == 3:
                    tt(p[1][:], p[1][:], p[3][:], ALU.add).then_inc(s["psum3a"], 1)
                    pool.wait_ge(s["psum3a"], t + 1)
                    tt(p[1][:], p[1][:], p[0][:], ALU.subtract).then_inc(s["psum3"], 1)
                else:
                    pool.wait_ge(s["w_rdy"], g + 1)
                    tt(p[k + 1][:], p[0][:], vel[:], ALU.add).then_inc(s["p_rdy"], 1)
                if k == 1:
                    pool.wait_ge(s["half_base"], g + 1)
                    pool.wait_ge(s["ref_rdy"], t + 1)
                    tt(ref[:], ref[:], drv[st][:], ALU.add).then_inc(s["ref2_rdy"], 1)
                    tt(drv[st][:], drv[st][:], q[0][:], ALU.subtract).then_inc(s["z_rdy"], 1)

            def send_rows(pos):
                pool.wait_ge(s["rows_rdy"], pos.tiles(1))
                pool.wait_ge(s["tags_rdy"], pos.tiles(1))
                pool.wait_ge(s["idx_rdy"], pos.tiles(1))
                pool.sem_inc(s["sending"], 1)
                for a in range(2):
                    pool.indirect_dma_start(
                        out=xs[:, :], out_offset=bass.IndirectOffsetOnAxis(ap=idx[:, a:a + 1], axis=0),
                        in_=io[:], in_offset=None).then_inc(s[f"sent{a + 1}"], 16)

            def fill_up(experts):
                for e in experts:
                    pool.indirect_dma_start(
                        out=xs[:, :], out_offset=bass.IndirectOffsetOnAxis(ap=fill_idx[:, e:e + 1], axis=0),
                        in_=io[:], in_offset=None).then_inc(s["filled_up"], 16)

            def add_result(pos, x):
                if pos.it is not None or pos.x0 + x > 0:
                    pool.wait_ge(s["y_free"], pos.xjobs(x, 16, 0))
                pool.wait_ge(s["y_rdy"], pos.xjobs(x, 1, 1))
                pool.sem_inc(s["sending"], 1)
                pool.indirect_dma_start(
                    out=out[:, :], out_offset=bass.IndirectOffsetOnAxis(ap=tok[x % 2][:, 0:1], axis=0),
                    in_=y[:], in_offset=None, compute_op=ALU.add).then_inc(s["y_free"], 16)

            def tile_part(pos, chain, weights, ffn, experts, before):
                for i in range(GS):
                    if chain:
                        stage(pos, i)
                    if weights:
                        for n in [n for n in PIECES_AT[i] if BY_POOL[n]]:
                            piece_lo(pool, pos, n)
                    if before and i == 0:
                        pool.wait_ge(s["stored"], pos.tiles(16))
                        add_result(pos, -2)
                    if before and i == 2:
                        add_result(pos, -1)
                    if ffn and i == 5:
                        send_rows(pos)
                    if not chain and i == 5:
                        pool.wait_ge(s["fill_in"], 16)
                        pool.wait_ge(s["fill_rdy"], 1)
                        fill_up(range(E // 2))

            tile_part(START, True, True, False, False, False)
            tile_part(FIRSTS, True, True, True, False, False)
            with pool.Fori(0, WTILES - 2) as it:
                tile_part(Pos(it=it, **TAKING), True, True, True, False, False)
            tile_part(BEFORE, True, False, True, False, False)
            tile_part(FIRSTX, True, False, True, True, False)
            with pool.Fori(0, NMAIN) as it:
                tile_part(Pos(it=it, **MAIN), True, False, True, True, True)
            tile_part(ENDING, False, False, True, True, True)
            pos = Pos(**TAIL)
            pool.wait_ge(s["stored"], 16 * (TILES + 1))
            add_result(pos, -2)
            fill_up(range(E // 2, E))
            add_result(pos, -1)
            add_result(pos, 0)
            with pool.Fori(0, NTAIL - 1) as it:
                for x in range(2):
                    add_result(Pos(it=it, **REST), x - 1)
            add_result(Pos(0, xjobs=SLOTS), -1)

        @block.scalar
        def _(act):
            def tanh_of(pos, i):
                g = pos.tiles(GS, 0, i)
                src = q[i % STAGES]
                act.wait_ge(s["q_rdy"], g + 1)
                act.activation(tanh, src[:], ACT.Tanh).then_inc(s["tanh_rdy"], 1)
                act.wait_ge(s["tanh_rdy"], g + 1)
                act.activation(th[:, 0], tanh, ACT.Copy, scale=ST).then_inc(s["th_rdy"], 1)
                act.activation(base[:], src[:], ACT.Square, scale=3.0 ** -0.5).then_inc(s["sq_rdy"], 1)

            def velocity(pos, i):
                g, k = pos.tiles(GS, 0, i), i % STAGES
                act.wait_ge(s["v_rdy"], g + 1)
                act.activation(vel[:], vel[:], ACT.Copy, scale=STEP[k] * EPS * BETA).then_inc(s["w_rdy"], 1)

            def third(pos, st):
                act.wait_ge(s["z_rdy"], pos.tiles(STEPS, 0, st + 1))
                act.activation(drv[st][:], drv[st][:], ACT.Copy, scale=1.0 / 3.0).then_inc(s["third_rdy"], 1)

            tanh_of(START, 0)
            for n, (_, cols, hi, _) in enumerate(first_pieces):
                act.wait_ge(s[f"w_in{n}"], 16)
                act.activation(hi, first_buf[n][:, 0:cols], ACT.Copy, scale=SW).then_inc(s["w_hi"], 1)

            def gate_of(pos, j):
                act.wait_ge(s["up_mm"], pos.jobs(j) + 1)
                act.activation(hid[:], ps_g[:, 0:H], ACT.Silu, scale=1.0 / (SW * SX)).then_inc(s["sg_rdy"], 1)

            def hidden_lead(pos, j):
                act.wait_ge(s["ht_mm"], pos.jobs(j) + 1)
                act.activation(ht[:, 0], ps_t[:], ACT.Copy).then_inc(s["hth_rdy"], 1)

            def scores(pos):
                act.wait_ge(s["lg_mm"], pos.tiles(1))
                act.activation(r["z"][:], ps_l[:, LOGIT], ACT.Copy, scale=1.0 / (SW * SX))
                act.activation(r["zt"][:], ps_l[:, LOGIT], ACT.Silu, scale=1.0 / (SW * SX))
                act.activation(r["sc"][:], ps_l[:, LOGIT], ACT.Tanh, scale=0.5 / (SW * SX)).then_inc(s["sc_rdy"], 1)

            def rows_of(pos):
                act.wait_ge(s["rows_mm"], pos.tiles(1))
                if pos.tile > 1:
                    act.wait_ge(s["sent1"], pos.tiles(16, -1))
                    act.wait_ge(s["sent2"], pos.tiles(16, -1))
                act.activation(io[:, 0:N].bitcast(F16), ps_x[:].rearrange("p a b -> p (a b)"),
                               ACT.Copy).then_inc(s["rows_rdy"], 1)

            def expert_x(pos, x):
                act.wait_ge(s["xt_mm"], pos.xjobs(x, 1, 1))
                act.activation(x_t[:].rearrange("p a b c -> p (a b) c"), ps_x[:], ACT.Copy).then_inc(s["x_t_rdy"], 1)

            def weighted(pos, x, j):
                act.wait_ge(s["y_mm"], pos.jobs(j) + 1)
                act.wait_ge(s[f"tag_in{x % 2}"], pos.pairs(x, 32, 32))
                if pos.it is not None or pos.x0 + x > 0:
                    act.wait_ge(s["y_free"], pos.xjobs(x, 16, 0))
                act.activation(y[:], ps_y[:], ACT.Identity, scale=ws[x % 2]).then_inc(s["y_rdy"], 1)

            def tile_part(pos, chain, weights, ffn, experts, before):
                for i in range(GS):
                    if chain and i % STAGES:
                        velocity(pos, i)
                    if before and i == 0:
                        hidden_lead(pos, -1)
                    if ffn and i in (1, 3):
                        gate_of(pos, i // 2)
                    if experts and i in (5, 7):
                        gate_of(pos, i // 2)
                    if ffn and i in (2, 4):
                        hidden_lead(pos, i // 2 - 1)
                    if experts and i == 6:
                        hidden_lead(pos, 2)
                    if chain and i % STAGES == 0:
                        velocity(pos, i)
                    if weights:
                        for n in PIECES_AT[i]:
                            piece_hi(act, pos, n)
                    if chain:
                        tanh_of(pos, i + 1)
                        if i % STAGES == 1:
                            third(pos, i // STAGES)
                        if i % STAGES == STAGES - 1:
                            st = i // STAGES
                            act.activation(qp[:, 0, :, st * B:(st + 1) * B], q[0][:], ACT.Copy,
                                           scale=SX).then_inc(s["qh_rdy"], 1)
                    if ffn and i == 0:
                        scores(pos)
                    if ffn and i == 1:
                        rows_of(pos)
                        if before:
                            weighted(pos, -1, -1)
                    if experts and i == 3:
                        expert_x(pos, 0)
                    if experts and i == 5:
                        expert_x(pos, 1)
                    if experts and i == 7:
                        weighted(pos, 0, 2)

            def tail_part(pos, final=False):
                for x in range(2):
                    gate_of(pos, x)
                    if not (final and x == 1):
                        expert_x(pos, x + 1)
                    weighted(pos, x - 1, x - 1)
                    hidden_lead(pos, x)

            tile_part(START, True, True, False, False, False)
            act.wait_ge(s["stored"], 16)
            tile_part(FIRSTS, True, True, True, False, False)
            with act.Fori(0, WTILES - 2) as it:
                tile_part(Pos(it=it, **TAKING), True, True, True, False, False)
            tile_part(BEFORE, True, False, True, False, False)
            tile_part(FIRSTX, True, False, True, True, False)
            with act.Fori(0, NMAIN) as it:
                tile_part(Pos(it=it, **MAIN), True, False, True, True, True)
            tile_part(ENDING, False, False, True, True, True)
            pos = Pos(**TAIL)
            hidden_lead(pos, -1)
            expert_x(pos, 0)
            tail_part(pos)
            with act.Fori(0, NTAIL - 2) as it:
                tail_part(Pos(it=it, **REST))
            tail_part(LASTS, True)
            weighted(Pos(0, jobs=TAIL["jobs"] + 2 * NTAIL, xjobs=SLOTS), -1, -1)

        @block.vector
        def _(dve):
            stt, tt = dve.scalar_tensor_tensor, dve.tensor_tensor
            dve.memset(ps_t[:], 0.0)
            dve.wait_ge(s["cond_in"], 16)
            dve.tensor_scalar(p[0][:], q[0][:], BETA, -ALPHA, ALU.mult, ALU.add).then_inc(s["p0_rdy"], 1)
            dve.tensor_scalar(q[0][:], q[0][:], 1.0, None, ALU.mult).then_inc(s["q_rdy"], 1)
            dve.wait_ge(s["consts_in"], 32)
            dve.tensor_scalar(bias_sb[:], bias_sb[:], -ALPHA / BETA, DT / 2, ALU.add, ALU.mult).then_inc(s["bias_rdy"], 1)
            dve.wait_ge(s["th_rdy"], 1)
            stt(th[:, 1], tanh, ST, th[:, 0], ALU.mult, ALU.subtract).then_inc(s["tl_rdy"], 1)
            for n, (_, cols, hi, lo) in enumerate(first_pieces):
                dve.wait_ge(s["w_hi"], n + 1)
                stt(lo, first_buf[n][:, 0:cols], SW, hi, ALU.mult, ALU.subtract).then_inc(s["w_lo"], 1)
            dve.wait_ge(s["bias_rdy"], 1)

            def next_tile(pos):
                return Pos(pos.tile + 1, it=pos.it)

            def drive_of(pos, st):
                dve.wait_ge(s[f"drv_in{st}"], pos.tiles(16, 0, 16))
                stt(drv[st][:], drv[st][:], DT / 2, bias_sb[:].rearrange("p (c o) -> p c o", o=1).to_broadcast([P, NC, B]),
                    ALU.mult, ALU.add).then_inc(s["d_rdy"], 1)

            def base_of(pos, i, ffn):
                k, st = i % STAGES, i // STAGES
                g, t = pos.tiles(GS, 0, i), pos.tiles(STEPS, 0, st)
                if k == 3:
                    dve.wait_ge(s["qsum"], 3 * t + 2)
                    stt(q[1][:], q[3][:], 1.0 / 3.0, q[1][:], ALU.mult, ALU.add).then_inc(s["qsum"], 1)
                dve.wait_ge(s["sq_rdy"], g + 1)
                stt(base[:], base[:], 1.0, q[k][:], ALU.subtract, ALU.mult).then_inc(s["cubic_rdy"], 1)
                if i == 0 and ffn:
                    end_of_tile(pos)
                if ffn:
                    routing(pos, ROUTE_AT[i][0])
                if k < 2:
                    dve.wait_ge(s["ref_rdy"], t + 1)
                elif k == 2:
                    dve.wait_ge(s["ref2_rdy"], t + 1)
                else:
                    dve.wait_ge(s["qsum"], 3 * t + 3)
                dve.wait_ge(s["cubic_rdy"], g + 1)
                stt(base[:], base[:], -STEP[k], (q[1] if k == 3 else ref)[:], ALU.mult,
                    ALU.add).then_inc(s["half_base"], 1)
                if ffn:
                    routing(pos, ROUTE_AT[i][1])
                p_ready(dve, pos, i)
                dve.wait_ge(s["half_base"], g + 1)
                stt(base[:], p[k][:], -STEP[k] / BETA, base[:], ALU.mult, ALU.add).then_inc(s["base_rdy"], 1)
                if k == 2:
                    stt(q[1][:], q[2][:], 2.0, q[1][:], ALU.mult, ALU.add).then_inc(s["qsum"], 1)

            def next_state(pos, i):
                k, st = i % STAGES, i // STAGES
                g, t = pos.tiles(GS, 0, i), pos.tiles(STEPS, 0, st)
                if k == 2:
                    dve.wait_ge(s["v_rdy"], g + 1)
                    dve.wait_ge(s["qsum"], 3 * t + 1)
                dve.wait_ge(s["base_rdy"], g + 1)
                dve.wait_ge(s["rk_mm"], g + 1)
                if k == 3:
                    stt(base[:], ps_rk[:], STEP[k] / (SW * ST), base[:], ALU.mult, ALU.add).then_inc(s["next_raw"], 1)
                    dve.wait_ge(s["next_raw"], t + 1)
                    dve.tensor_scalar(q[0][:], base[:], -CLAMP, CLAMP, ALU.max, ALU.min).then_inc(s["q_rdy"], 1)
                else:
                    stt(q[k + 1][:], ps_rk[:], STEP[k] / (SW * ST), base[:], ALU.mult, ALU.add).then_inc(s["q_rdy"], 1)

            def sums(pos, i):
                k, st = i % STAGES, i // STAGES
                g, t = pos.tiles(GS, 0, i), pos.tiles(STEPS, 0, st)
                if k == 1:
                    dve.wait_ge(s["p_rdy"], pos.tiles(3 * STEPS, 0, 3 * st + 2))
                    stt(p[1][:], p[2][:], 2.0, p[1][:], ALU.mult, ALU.add).then_inc(s["psum1"], 1)
                if k == 2:
                    dve.wait_ge(s["third_rdy"], t + 1)
                    stt(q[1][:], q[1][:], 1.0 / 3.0, drv[st][:], ALU.mult, ALU.add).then_inc(s["qsum"], 1)
                if k == 3:
                    dve.wait_ge(s["psum3"], t + 1)
                    dve.wait_ge(s["w_rdy"], g + 1)
                    stt(p[1][:], p[1][:], 1.0 / 3.0, vel[:], ALU.mult, ALU.add).then_inc(s["psum4"], 1)
                    dve.wait_ge(s["psum4"], t + 1)
                    dve.tensor_scalar(p[0][:], p[1][:], -CLAMP * BETA - ALPHA, CLAMP * BETA - ALPHA, ALU.max,
                                      ALU.min).then_inc(s["p0_rdy"], 1)

            def tanh_rest(pos, i):
                dve.wait_ge(s["th_rdy"], pos.tiles(GS, 0, i + 2))
                stt(th[:, 1], tanh, ST, th[:, 0], ALU.mult, ALU.subtract).then_inc(s["tl_rdy"], 1)

            def state_rest(pos, st, off=0):
                cols = slice(st * B, (st + 1) * B)
                dve.wait_ge(s["qh_rdy"], pos.tiles(STEPS, off, st + 1))
                stt(qp[:, 1, :, cols], q[0][:], SX, qp[:, 0, :, cols], ALU.mult, ALU.subtract).then_inc(s["qp_rdy"], 1)

            def end_of_tile(pos):
                state_rest(pos, STEPS - 1, -1)
                if pos.tile > 1:
                    list_out(pos, -1)

            def routing(pos, numbers, skipped=0):
                lo, key, sc, z, zt, o1, o2 = (r[k][:] for k in "lo key sc z zt o1 o2".split())
                slot, nf, eq = lo, zt, key
                new = pre[0][:, 4:]
                for n in numbers:
                    if n > skipped:
                        dve.wait_ge(s["route"], pos.tiles(NROUTE, -1, n - skipped))
                    if n == 0:
                        dve.wait_ge(s["sc_rdy"], pos.tiles(1))
                        ins = dve.tensor_scalar(lo, z, -1.0, None, ALU.min)
                    if n == 1:
                        ins = dve.reciprocal(lo, lo)
                    if n == 2:
                        ins = tt(lo, zt, lo, ALU.mult)
                    if n == 3:
                        ins = stt(lo, z, -1.0, lo, ALU.is_lt, ALU.mult)
                    if n == 4:
                        ins = dve.tensor_scalar(sc, sc, 0.5, 0.5, ALU.mult, ALU.add)
                    if n == 5:
                        ins = stt(sc, z, -1.0, sc, ALU.is_ge, ALU.mult)
                    if n == 6:
                        ins = tt(sc, sc, lo, ALU.add)
                    if n == 7:
                        ins = tt(lo, sc, gb[:], ALU.add)
                    if n in (8, 13):
                        ins = dve.tensor_reduce(mx, lo, AXIS.X, ALU.max)
                    if n in (9, 14):
                        ins = stt(key, lo, mx, desc[:], ALU.is_equal, ALU.mult)
                    if n in (10, 15):
                        ins = dve.tensor_reduce(ix, key, AXIS.X, ALU.max)
                    if n in (11, 16):
                        ins = dve.tensor_scalar(o1 if n == 11 else o2, desc[:], ix, None, ALU.is_equal)
                    if n == 12:
                        ins = stt(lo, o1, -1e30, lo, ALU.mult, ALU.add)
                    if n == 17:
                        ins = tt(chosen[:], o1, o2, ALU.add)
                    if n == 18:
                        ins = tt(key, chosen[:], sc, ALU.mult)
                    if n == 19:
                        ins = dve.tensor_reduce(mx, key, AXIS.X, ALU.add)
                    if n == 20:
                        ins = dve.reciprocal(ix, mx)
                    if n == 21:
                        if pos.tile > 1:
                            dve.wait_ge(s["sent1"], pos.tiles(16, -1))
                            dve.wait_ge(s["sent2"], pos.tiles(16, -1))
                        dve.tensor_scalar(io[:, N + 1:], key, ix, 1.0 / (SW * SH), ALU.mult, ALU.mult)
                        dve.tensor_copy(io[:, N:N + 1].bitcast(I32), part).then_inc(s["tags_rdy"], 1)
                        ins = dve.tensor_scalar(part, part, float(P), None, ALU.add)
                    if n == 22:
                        dve.wait_ge(s["rank_mm"], pos.tiles(1))
                        ins = tt(slot, count[:], ps_l[:, RANK], ALU.add)
                    if n == 23:
                        ins = tt(zt, o1, slot, ALU.mult)
                    if n == 24:
                        dve.tensor_reduce(idx[:, 0:1], zt, AXIS.X, ALU.max)
                        ins = tt(key, o2, slot, ALU.mult)
                    if n == 25:
                        dve.tensor_reduce(idx[:, 1:2], key, AXIS.X, ALU.max).then_inc(s["idx_rdy"], 1)
                        ins = tt(count[:], count[:], ps_l[:, TOTAL], ALU.add)
                    if n == 26:
                        ins = tt(rem[:], rem[:], ps_l[:, TOTAL], ALU.add)
                    if n == 27:
                        ins = dve.tensor_scalar(new, rem[:], float(P), None, ALU.is_ge)
                    if n == 28:
                        ins = stt(rem[:], new, -float(P), rem[:], ALU.mult, ALU.add)
                    if n == ENTER:
                        ins = tt(pre[1][:, 4:], new, pre[0][:, 3:3 + E], ALU.add)
                    if n == 30:
                        ins = tt(pre[2][:, 4:], pre[1][:, 4:], pre[1][:, 2:2 + E], ALU.add)
                    if n == 31:
                        ins = tt(nf, pre[2][:, 4:], pre[2][:, 0:E], ALU.add)
                    if n == 32:
                        ins = stt(eq, nf, filled, new, ALU.add, ALU.subtract)
                    if n == 33:
                        ins = stt(eq, eq, slots_of, new, ALU.is_equal, ALU.mult)
                    if n == 34:
                        ins = tt(slot, eq, code[:], ALU.mult)
                    if n == 35:
                        ins = dve.tensor_reduce(lv[:, 0:1], slot, AXIS.X, ALU.add)
                    if n == 36:
                        ins = tt(slot, eq, eidx[:], ALU.mult)
                    if n == 37:
                        ins = dve.tensor_reduce(lv[:, 1:2], slot, AXIS.X, ALU.add)
                    if n == 38:
                        ins = tt(filled, filled, nf[:, E - 1:E], ALU.add)
                    if n == 39:
                        ins = stt(code[:], new, float(P), code[:], ALU.mult, ALU.add)
                    ins.then_inc(s["route"], 1)
                    if n == NROUTE - 1:
                        tt(lst, lst, lv, ALU.add).then_inc(s["list_rdy"], 1)

            def list_out(pos, off=0):
                dve.wait_ge(s["list_mm"], pos.tiles(1, off))
                dve.tensor_copy(todo[:], ps_l[0:1, LIST:LIST + 2 * SLOTS]).then_inc(s["todo_rdy"], 1)

            def hidden(pos, j):
                dve.wait_ge(s["sg_rdy"], pos.jobs(j) + 1)
                stt(hid[:], ps_u[:, 0:H], SH / (SW * SX), hid[:], ALU.mult, ALU.mult).then_inc(s["h_rdy"], 1)

            def hidden_rest(pos, j):
                dve.wait_ge(s["hth_rdy"], pos.jobs(j) + 1)
                tt(ht[:, 1], ps_t[:], ht[:, 0], ALU.subtract).then_inc(s["hts_rdy"], 1)

            def shared_out(pos):
                dve.wait_ge(s["y_mm"], pos.jobs(1) + 1)
                dve.wait_ge(s["res_in"], pos.tiles(16))
                stt(res[:], ps_y[:], 1.0 / (SW * SH), res[:], ALU.mult, ALU.add).then_inc(s["res_rdy"], 1)

            def tile_part(pos, chain, weights, ffn, experts, before=False, more=True):
                for i in range(GS):
                    if chain:
                        base_of(pos, i, ffn)
                    elif ffn:
                        if i == 0:
                            end_of_tile(pos)
                        for at in ROUTE_AT[i][:2]:
                            routing(pos, at)
                    if chain and i == STAGES:
                        state_rest(pos, 0)
                    if ffn and i == 3 or experts and i == 7:
                        hidden(pos, i // 2)
                    if ffn:
                        routing(pos, ROUTE_AT[i][2])
                    if weights:
                        for n in [n for n in PIECES_AT[i] if not BY_POOL[n]][:-1 if i in SPLIT_LATE else None]:
                            piece_lo(dve, pos, n)
                    if ffn and i == 6:
                        shared_out(pos)
                    if chain:
                        next_state(pos, i)
                    if ffn:
                        routing(pos, ROUTE_AT[i][3])
                    if chain:
                        sums(pos, i)
                        if i == 0:
                            drive_of(pos, 1)
                        if i == STAGES and more:
                            drive_of(next_tile(pos), 0)
                    if ffn and i == 1 or experts and i == 5:
                        hidden(pos, i // 2)
                    if weights and i in SPLIT_LATE:
                        piece_lo(dve, pos, [n for n in PIECES_AT[i] if not BY_POOL[n]][-1])
                    if before and i == 0:
                        hidden_rest(pos, -1)
                    if ffn and i in (2, 4):
                        hidden_rest(pos, i // 2 - 1)
                    if experts and i == 6:
                        hidden_rest(pos, 2)
                    if chain:
                        tanh_rest(pos, i)
                    if ffn:
                        routing(pos, ROUTE_AT[i][4])
                    if not chain and i == 5:
                        dve.tensor_scalar(fill_idx[:], count[:], slots_of, None, ALU.add).then_inc(s["fill_rdy"], 1)

            def tail_part(pos, flush=False):
                for x in range(2):
                    if flush and x == 1:
                        list_out(ENDING, 1)
                    hidden(pos, x)
                    hidden_rest(pos, x)

            dve.wait_ge(s["set_up"], 1)
            drive_of(START, 0)
            tile_part(START, True, True, False, False)
            dve.wait_ge(s["stored"], 16)
            tile_part(FIRSTS, True, True, True, False)
            with dve.Fori(0, WTILES - 2) as it:
                tile_part(Pos(it=it, **TAKING), True, True, True, False)
            tile_part(BEFORE, True, False, True, False)
            tile_part(FIRSTX, True, False, True, True)
            with dve.Fori(0, NMAIN - 1) as it:
                tile_part(Pos(it=it, **MAIN), True, False, True, True, True)
            tile_part(MAINEND, True, False, True, True, True, False)
            tile_part(ENDING, False, False, True, True, True)
            list_out(ENDING)
            pos = Pos(**TAIL)
            hidden_rest(pos, -1)
            dve.wait_ge(s["todo_rdy"], TILES)
            dve.tensor_scalar(pre[0][:, 4:], rem[:], 0.5, None, ALU.is_ge).then_inc(s["route"], 1)
            routing(Pos(TILES + 1), range(ENTER, NROUTE), ENTER - 1)
            tail_part(pos, True)
            with dve.Fori(0, NTAIL - 1) as it:
                tail_part(Pos(it=it, **REST))

        @block.tensor
        def _(pe):
            mm = pe.matmul

            def chain_of(pos, i):
                pe.wait_ge(s["th_rdy"], pos.tiles(GS, 0, i + 1))
                for o in range(NC):
                    for k in range(NC):
                        hi, lo = (cw[:, a, k, o * P:(o + 1) * P] for a in range(2))
                        mm(ps_rk[:, o], lo, th[:, 0, k], start=o == k == 0, stop=False)
                        mm(ps_rk[:, o], hi, th[:, 0, k], start=False, stop=False)
                pe.wait_ge(s["tl_rdy"], pos.tiles(GS, 0, i + 1))
                for o in range(NC):
                    for k in range(NC):
                        last = mm(ps_rk[:, o], cw[:, 0, k, o * P:(o + 1) * P], th[:, 1, k], start=False,
                                  stop=o == k == NC - 1)
                last.then_inc(s["rk_mm"], 1)

            PAIRS = ((0, 0), (0, 1), (1, 0))

            def router(pos):
                pe.wait_ge(s["qp_rdy"], pos.tiles(STEPS))
                for k in range(NC):
                    for a, b in PAIRS:
                        last = mm(ps_l[:, LOGIT], qp[:, a, k], gw[:, b, k], start=k == 0 and a == b,
                                  stop=k == NC - 1 and a == 1)
                last.then_inc(s["lg_mm"], 1)

            def up_of(pos, j, x, weights):
                for k in range(NC):
                    for a, b in PAIRS:
                        for half, ps in enumerate((ps_g, ps_u)):
                            last = mm(ps[:, 0:H], x[:, a, k], weights(P, b, (2 * k + half) * H, H),
                                      start=k == 0 and a == b, stop=k == NC - 1 and a == 1)
                last.then_inc(s["up_mm"], 1)

            def turn_of(pos, j):
                pe.wait_ge(s["h_rdy"], pos.jobs(j) + 1)
                for k, (h0, hn) in enumerate(HK):
                    last = pe.transpose(ps_t[0:hn, k], hid[:, h0:h0 + hn], ident[:])
                last.then_inc(s["ht_mm"], 1)

            def down_of(pos, j, weights, first=True, final=True):
                pe.wait_ge(s["hts_rdy"], pos.jobs(j) + 1)
                for k, (_, hn) in enumerate(HK):
                    for a, b in PAIRS:
                        last = mm(ps_y[:], ht[0:hn, a, k], weights(hn, b, UP + k * N, N),
                                  start=first and k == 0 and a == b, stop=final and k == len(HK) - 1 and a == 1)
                last.then_inc(s["y_mm"], 1)

            def shared(a):
                return lambda pp, b, c, n: w[0:pp, E + a, b, c:c + n]

            def expert(e):
                return lambda pp, b, c, n: w[0:pp, bass.ds(e, 1), b, c:c + n].rearrange("p o c -> p (o c)")

            def rows_turn(pos):
                for a in range(2):
                    for k in range(NC):
                        last = pe.transpose(ps_x[:, a * NC + k], qp[:, a, k], ident16[:])
                last.then_inc(s["rows_mm"], 1)

            def expert_turn(pos, x):
                pe.wait_ge(s["x_in_rdy"], pos.xjobs(x, 16, 16))
                for c in range(2 * NC):
                    last = pe.transpose(ps_x[:, c], x_in[:, 0:N].bitcast(F16)[:, c * P:(c + 1) * P], ident16[:])
                last.then_inc(s["xt_mm"], 1)

            def ranks(pos):
                pe.wait_ge(s["tags_rdy"], pos.tiles(1))
                mm(ps_l[:, RANK], upper[:], chosen[:], start=True, stop=True)
                mm(ps_l[:, TOTAL], ones[:], chosen[:], start=True, stop=True).then_inc(s["rank_mm"], 1)

            def list_row(pos, off=0):
                pe.wait_ge(s["list_rdy"], pos.tiles(1, off))
                for c in range(2):
                    last = mm(ps_l[0:1, LIST + c * SLOTS:LIST + (c + 1) * SLOTS], lst[:, c:c + 1], ident[:, 0:SLOTS],
                              start=True, stop=True)
                last.then_inc(s["list_mm"], 1)

            def experts_of(pos, x0, x1=2):
                at, n = pos.xjobs(x0, 1, SLOTS), x1 - x0
                _, found = nc.values_load_multi_w_load_instructions(
                    todo[0:1, bass.ds(at, n)] if pos.it is not None else todo[0:1, at:at + n],
                    engines=[mybir.EngineType.PE], min_val=0, max_val=E - 1)
                return dict(zip(range(x0, x1), found))

            def tile_part(pos, chain, ffn, experts, before, last=False):
                for i in range(GS):
                    if chain:
                        chain_of(pos, i)
                    if ffn and i == 0:
                        if pos.tile > 1:
                            pe.wait_ge(s["todo_rdy"], pos.tiles(1, -1))
                        router(pos)
                        if experts:
                            e = experts_of(pos, -1 if before else 0, 3 if last else 2)
                        up_of(pos, 0, qp, shared(0))
                    if ffn and i == 1:
                        rows_turn(pos)
                        if before:
                            pe.wait_ge(s["y_rdy"], pos.xjobs(-1))
                            down_of(pos, -1, expert(e[-1]))
                        turn_of(pos, 0)
                    if ffn and i == 2:
                        up_of(pos, 1, qp, shared(1))
                    if ffn and i == 3:
                        if experts:
                            pe.wait_ge(s["rows_rdy"], pos.tiles(1))
                            expert_turn(pos, 0)
                        if before:
                            pe.wait_ge(s["y_rdy"], pos.xjobs(0))
                        down_of(pos, 0, shared(0), final=False)
                        turn_of(pos, 1)
                    if experts and i == 4:
                        pe.wait_ge(s["x_t_rdy"], pos.xjobs(0, 1, 1))
                        up_of(pos, 2, x_t, expert(e[0]))
                    if ffn and i == 4:
                        ranks(pos)
                    if experts and i == 5:
                        expert_turn(pos, 1)
                    if ffn and i == 5:
                        down_of(pos, 1, shared(1), first=False)
                    if experts and i == 5:
                        turn_of(pos, 2)
                    if experts and i == 6:
                        pe.wait_ge(s["x_t_rdy"], pos.xjobs(1, 1, 1))
                        up_of(pos, 3, x_t, expert(e[1]))
                    if experts and i == 7:
                        pe.wait_ge(s["res_rdy"], pos.tiles(1))
                        down_of(pos, 2, expert(e[0]))
                        turn_of(pos, 3)
                    if ffn and i == 7:
                        list_row(pos)
                    if last and i == 7:
                        expert_turn(pos, 2)
                return e if last else None

            def tail_part(pos, e, final=False):
                for x in range(2):
                    pe.wait_ge(s["x_t_rdy"], pos.xjobs(x, 1, 1))
                    up_of(pos, x, x_t, expert(e[x]))
                    if not (final and x == 1):
                        expert_turn(pos, x + 1)
                    pe.wait_ge(s["y_rdy"], pos.xjobs(x - 1))
                    down_of(pos, x - 1, expert(e[x - 1]))
                    turn_of(pos, x)

            pe.wait_ge(s["set_up"], 1)
            all_split(pe, 0)
            tile_part(START, True, False, False, False)
            all_split(pe, 1)
            tile_part(FIRSTS, True, True, False, False)
            with pe.Fori(0, WTILES - 2) as it:
                tile_part(Pos(it=it, **TAKING), True, True, False, False)
            tile_part(BEFORE, True, True, False, False)
            all_split(pe, WTILES)
            tile_part(FIRSTX, True, True, True, False)
            with pe.Fori(0, NMAIN) as it:
                tile_part(Pos(it=it, **MAIN), True, True, True, True)
            e = tile_part(ENDING, False, True, True, True, True)
            pos = Pos(**TAIL)
            e = {x - 2: number for x, number in e.items()}
            pe.wait_ge(s["x_t_rdy"], pos.xjobs(0, 1, 1))
            up_of(pos, 0, x_t, expert(e[0]))
            pe.wait_ge(s["todo_rdy"], TILES)
            e.update(experts_of(pos, 1))
            expert_turn(pos, 1)
            pe.wait_ge(s["y_rdy"], pos.xjobs(-1))
            down_of(pos, -1, expert(e[-1]))
            turn_of(pos, 0)
            list_row(ENDING, 1)
            pe.wait_ge(s["x_t_rdy"], pos.xjobs(1, 1, 1))
            up_of(pos, 1, x_t, expert(e[1]))
            pe.wait_ge(s["y_rdy"], pos.xjobs(0))
            down_of(pos, 0, expert(e[0]))
            turn_of(pos, 1)
            pe.wait_ge(s["todo_rdy"], TILES + 1)
            expert_turn(pos, 2)
            with pe.Fori(0, NTAIL - 2) as it:
                pos = Pos(it=it, **REST)
                tail_part(pos, experts_of(pos, -1))
            e = experts_of(LASTS, -1)
            tail_part(LASTS, e, True)
            end = Pos(0, jobs=TAIL["jobs"] + 2 * NTAIL, xjobs=SLOTS)
            pe.wait_ge(s["y_rdy"], SLOTS - 1)
            down_of(end, -1, expert(e[1]))


def kernel(x, cond_2048, L0_cond_coupling, L0_cond_bias, L0_ffn_gate_w, L0_ffn_gate_bias, L0_ffn_shared_gw,
           L0_ffn_shared_dw, L0_ffn_up_w, L0_ffn_down_w):
    import concourse.bacc as _bacc
    from concourse.bass_utils import run_bass_kernel_spmd as _run

    def split(a, n):
        return np.ascontiguousarray(a.reshape(n, P, -1).transpose(1, 0, 2))

    x, cond_2048 = np.asarray(x), np.asarray(cond_2048)
    xt = x.transpose(1, 0, 2)
    sg, sd = np.asarray(L0_ffn_shared_gw), np.asarray(L0_ffn_shared_dw)
    ups = [np.asarray(u) for u in np.asarray(L0_ffn_up_w)]
    downs = [np.asarray(d) for d in np.asarray(L0_ffn_down_w)]
    for i in range(2):
        half = slice(i * H, (i + 1) * H)
        ups.append(np.concatenate([sg[2 * H:][half], sg[:2 * H][half]]))
        downs.append(sd[:, half])
    arrays = {
        "in_drive": np.ascontiguousarray(xt.reshape(T, B, NC, P).transpose(0, 3, 2, 1)),
        "in_cond": np.ascontiguousarray(cond_2048.reshape(B, NC, P).transpose(2, 1, 0)),
        "in_rows": np.ascontiguousarray(xt.reshape(T * B, N)),
        "in_coupling": split(np.asarray(L0_cond_coupling).T, NC),
        "in_bias": np.ascontiguousarray(np.asarray(L0_cond_bias).reshape(NC, P).T),
        "in_gate": split(np.asarray(L0_ffn_gate_w).T, NC).reshape(P, NC * E),
        "in_gate_bias": np.ascontiguousarray(np.asarray(L0_ffn_gate_bias)),
        "in_up": np.stack([split(u.T, NC).reshape(P, UP) for u in ups]),
        "in_down": np.stack([np.ascontiguousarray(d.T) for d in downs]),
    }
    nc = _bacc.Bacc("TRN2", target_bir_lowering=False, num_devices=1)
    aps = [nc.dram_tensor(n, a.shape, F32, kind="ExternalInput").ap() for n, a in arrays.items()]
    out = nc.dram_tensor("result", (TOKENS + P, N), F32, kind="ExternalOutput").ap()
    xs = nc.dram_tensor("expert_rows", (NO_ROWS + P, ROW), F32, kind="Internal").ap()
    build(nc, *aps, out, xs)
    r = _run(nc, [arrays], core_ids=[0])
    return np.ascontiguousarray(r.results[0]["result"][:TOKENS].reshape(T, B, N).transpose(1, 0, 2))
```
